# Optimizing a Trainium2 kernel written in Bass

```python
import numpy as np
import jax
import jax.numpy as jnp

def _softmax(x, axis=-1):
    return jax.nn.softmax(x, axis=axis)

def _gelu(x):
    return jax.nn.gelu(x, approximate=True)

def _silu(x):
    return jax.nn.silu(x)

def _sigmoid(x):
    return jax.nn.sigmoid(x)

def _layernorm(x, axis=-1, eps=1e-05):
    m = jnp.mean(x, axis=axis, keepdims=True)
    v = jnp.var(x, axis=axis, keepdims=True)
    return (x - m) / jnp.sqrt(v + eps)

def _scatter_add(tgt, idx, src, axis=0):
    return tgt.at[idx].add(src)

def _segment_sum(src, seg, n):
    return jax.ops.segment_sum(src, seg, n)
kernel_name = 'mk_adj_preln_d1_adj_r2_369c6d'

def setup_inputs(seed: int=0):
    np.random.seed(seed)
    _w = jnp.asarray

    def _rec_inputs():
        import jax
        import jax.numpy as jnp
        _gk = jax.random.key(seed)
        x = 7.22e-05 + 1 * jax.random.normal(jax.random.fold_in(_gk, 1), (64, 128, 128), jnp.float32)
        _w = (1.0 + jnp.arange(128, dtype=jnp.float32)) ** (-0.5)
        _w = _w / _w.mean()
        _pij = jnp.clip(0.125 * _w[:, None] * _w[None, :], 0.0, 1.0)
        _a = jax.random.uniform(jax.random.fold_in(_gk, 2), (64, 128, 128)) < _pij
        _a = jnp.logical_or(_a, jnp.swapaxes(_a, -1, -2))
        _a = jnp.logical_or(_a, jnp.eye(128, dtype=bool))
        _af = _a.astype(jnp.float32)
        adj = _af
        return (x, adj)
    x, adj = _rec_inputs()

    def _L0_gnn_setup():
        import jax, jax.numpy as jnp
        import numpy as np
        from jax import lax
        DIM = 128
        EPS = 1e-05

        def _bn(h, g, b, m, v):
            scale = g / jnp.sqrt(v + EPS)
            return h * scale[None, :, None] + (b - m * scale)[None, :, None]

        def _conv1d(h, w, pad):
            return lax.conv_general_dilated(h, w, window_strides=(1,), padding=[(pad, pad)], dimension_numbers=('NCH', 'OIH', 'NCH'))
        key = jax.random.key(seed)
        ks = jax.random.split(key, 16)
        bs, n, d = (16, 1024, DIM)
        s = 0.05
        return {'x': jax.random.normal(ks[0], (bs, n, d), jnp.float32), 'mask': jnp.ones((bs, n, n), jnp.float32), 'w_se': jax.random.normal(ks[1], (3, d), jnp.float32) * s, 'b_se': jnp.zeros((3,), jnp.float32), 'conv1_w': jax.random.normal(ks[2], (d, d, 1), jnp.float32) * s, 'bn1_g': jnp.ones((d,), jnp.float32), 'bn1_b': jnp.zeros((d,), jnp.float32), 'bn1_m': jnp.zeros((d,), jnp.float32), 'bn1_v': jnp.ones((d,), jnp.float32), 'conv2_w': jax.random.normal(ks[3], (d, d, 17), jnp.float32) * s, 'bn2_g': jnp.ones((d,), jnp.float32), 'bn2_b': jnp.zeros((d,), jnp.float32), 'bn2_m': jnp.zeros((d,), jnp.float32), 'bn2_v': jnp.ones((d,), jnp.float32), 'w_msg': jax.random.normal(ks[4], (d, d), jnp.float32) * s, 'b_msg': jnp.zeros((d,), jnp.float32), 'w_ih': jax.random.normal(ks[5], (3 * d, 2 * d), jnp.float32) * s, 'b_ih': jnp.zeros((3 * d,), jnp.float32), 'w_hh': jax.random.normal(ks[6], (3 * d, d), jnp.float32) * s, 'b_hh': jnp.zeros((3 * d,), jnp.float32)}
    _L0_gnn_all = _L0_gnn_setup()
    _L0_gnn_in = {k: v for k, v in _L0_gnn_all.items() if k in ('w_se', 'b_se', 'conv1_w', 'bn1_g', 'bn1_b', 'bn1_m', 'bn1_v', 'conv2_w', 'bn2_g', 'bn2_b', 'bn2_m', 'bn2_v', 'w_msg', 'b_msg', 'w_ih', 'b_ih', 'w_hh', 'b_hh')}
    del _L0_gnn_all
    return {'x': x, 'adj': adj, 'L0_gnn_w_se': _L0_gnn_in['w_se'], 'L0_gnn_b_se': _L0_gnn_in['b_se'], 'L0_gnn_conv1_w': _L0_gnn_in['conv1_w'], 'L0_gnn_bn1_g': _L0_gnn_in['bn1_g'], 'L0_gnn_bn1_b': _L0_gnn_in['bn1_b'], 'L0_gnn_bn1_m': _L0_gnn_in['bn1_m'], 'L0_gnn_bn1_v': _L0_gnn_in['bn1_v'], 'L0_gnn_conv2_w': _L0_gnn_in['conv2_w'], 'L0_gnn_bn2_g': _L0_gnn_in['bn2_g'], 'L0_gnn_bn2_b': _L0_gnn_in['bn2_b'], 'L0_gnn_bn2_m': _L0_gnn_in['bn2_m'], 'L0_gnn_bn2_v': _L0_gnn_in['bn2_v'], 'L0_gnn_w_msg': _L0_gnn_in['w_msg'], 'L0_gnn_b_msg': _L0_gnn_in['b_msg'], 'L0_gnn_w_ih': _L0_gnn_in['w_ih'], 'L0_gnn_b_ih': _L0_gnn_in['b_ih'], 'L0_gnn_w_hh': _L0_gnn_in['w_hh'], 'L0_gnn_b_hh': _L0_gnn_in['b_hh']}

def reference(x, adj, L0_gnn_w_se, L0_gnn_b_se, L0_gnn_conv1_w, L0_gnn_bn1_g, L0_gnn_bn1_b, L0_gnn_bn1_m, L0_gnn_bn1_v, L0_gnn_conv2_w, L0_gnn_bn2_g, L0_gnn_bn2_b, L0_gnn_bn2_m, L0_gnn_bn2_v, L0_gnn_w_msg, L0_gnn_b_msg, L0_gnn_w_ih, L0_gnn_b_ih, L0_gnn_w_hh, L0_gnn_b_hh):
    import jax
    import jax.numpy as jnp

    def _L0_gnn_ref(x, mask, w_se, b_se, conv1_w, bn1_g, bn1_b, bn1_m, bn1_v, conv2_w, bn2_g, bn2_b, bn2_m, bn2_v, w_msg, b_msg, w_ih, b_ih, w_hh, b_hh):
        import jax, jax.numpy as jnp
        import numpy as np
        from jax import lax
        DIM = 128
        EPS = 1e-05

        def _bn(h, g, b, m, v):
            scale = g / jnp.sqrt(v + EPS)
            return h * scale[None, :, None] + (b - m * scale)[None, :, None]

        def _conv1d(h, w, pad):
            return lax.conv_general_dilated(h, w, window_strides=(1,), padding=[(pad, pad)], dimension_numbers=('NCH', 'OIH', 'NCH'))
        d = x.shape[-1]
        xc = jnp.transpose(x, (0, 2, 1))
        h = _bn(_conv1d(xc, conv1_w, 0), bn1_g, bn1_b, bn1_m, bn1_v)
        h = jax.nn.relu(h)
        h = _bn(_conv1d(h, conv2_w, 8), bn2_g, bn2_b, bn2_m, bn2_v)
        x_conv = jnp.transpose(jax.nn.relu(h + xc), (0, 2, 1))
        s = x @ w_se.T + b_se
        sq = jnp.sum(s * s, axis=-1)
        dist = sq[:, :, None] + sq[:, None, :] - 2.0 * jnp.einsum('bnd,bmd->bnm', s, s)
        A = jnp.exp(-dist) * mask
        msg = jax.nn.relu(x @ w_msg.T + b_msg)
        x_nmp = jnp.einsum('bnm,bmd->bnd', A, msg)
        x_in = jnp.concatenate([x_conv, x_nmp], axis=-1)
        gi = x_in @ w_ih.T + b_ih
        gh = x @ w_hh.T + b_hh
        gi_r, gi_z, gi_n = (gi[..., :d], gi[..., d:2 * d], gi[..., 2 * d:])
        gh_r, gh_z, gh_n = (gh[..., :d], gh[..., d:2 * d], gh[..., 2 * d:])
        r = jax.nn.sigmoid(gi_r + gh_r)
        z = jax.nn.sigmoid(gi_z + gh_z)
        nn_ = jnp.tanh(gi_n + r * gh_n)
        return (1.0 - z) * nn_ + z * x
    h = jnp.maximum(_layernorm(x, axis=-1), 0.0)
    x = x + _L0_gnn_ref(h, adj, L0_gnn_w_se, L0_gnn_b_se, L0_gnn_conv1_w, L0_gnn_bn1_g, L0_gnn_bn1_b, L0_gnn_bn1_m, L0_gnn_bn1_v, L0_gnn_conv2_w, L0_gnn_bn2_g, L0_gnn_bn2_b, L0_gnn_bn2_m, L0_gnn_bn2_v, L0_gnn_w_msg, L0_gnn_b_msg, L0_gnn_w_ih, L0_gnn_b_ih, L0_gnn_w_hh, L0_gnn_b_hh)
    return x

_drawn_inputs = setup_inputs


def setup_inputs(seed=0):
    import zlib

    import numpy as np

    out = dict(_drawn_inputs(seed))
    spreads = {'L0_gnn_b_se': (0.0, 0.8),
     'L0_gnn_bn1_g': (1.0, 0.6),
     'L0_gnn_bn1_b': (0.0, 0.481),
     'L0_gnn_bn1_m': (0.0, 0.454),
     'L0_gnn_bn1_v': (1.0, 0.6),
     'L0_gnn_bn2_g': (1.0, 0.6),
     'L0_gnn_bn2_b': (0.0, 0.748),
     'L0_gnn_bn2_m': (0.0, 0.692),
     'L0_gnn_bn2_v': (1.0, 0.6),
     'L0_gnn_b_msg': (0.0, 0.1),
     'L0_gnn_b_ih': (0.0, 0.28),
     'L0_gnn_b_hh': (0.0, 0.384)}
    factors = {}
    for name, (base, spread) in spreads.items():
        noise = np.random.default_rng([zlib.crc32(name.encode()), seed]).standard_normal(out[name].shape)
        drawn = base * np.exp(spread * noise) if base else spread * noise
        out[name] = jnp.asarray(drawn.astype(out[name].dtype))
    for name, factor in factors.items():
        out[name] = (out[name] * factor).astype(out[name].dtype)
    return out
```

```python
from contextlib import ExitStack

import concourse.bass as bass
from concourse import mybir

F32 = mybir.dt.float32
F32R = mybir.dt.float32r
ALU = mybir.AluOpType
ACT = mybir.ActivationFunctionType

P = 128
NB = 64
GB = 8
CB = 4
NCH = GB // CB
NG = NB // GB
CW = CB * P
GW = GB * P
TAPS = 17
EPS = 1e-5

CPAD, UPAD, VPAD = P + 8, P // 2 + 4, P // 4 + 4
HALF, QUART = P // 2, P // 4
ORDER = "bac"
LEN1 = {"a": (TAPS + 1) // 2, "b": (TAPS + 1) // 2, "c": TAPS // 2}


def sub_taps():
    at, out = 0, []
    for u in ORDER:
        for v in ORDER:
            n = LEN1[u] // 2 if v == "c" else (LEN1[u] + 1) // 2
            out.append((at, n))
            at += n
    return out, at


SUBS, NT = sub_taps()
CONV1, MSG = NT, NT + 1
def IH(gate, part):
    return NT + 2 + 2 * gate + part
def HH(gate):
    return NT + 8 + gate
SE = NT + 11
NBLK = NT + 12
R, Z, N = 0, 1, 2
S_ROWS = (0, 32, 64)
SK = 67
(G1, B1, M1, V1, G2, B2, M2, V2, BIR, BIZ, BIN, BHR, BHZ, BHN,
 SC1, SC2, C1B, C2B, HR, HZ, HN, T1, T2) = range(23)


def gnn_kernel(nc, x, adj, w_se, b_se, conv1_w, bn1_g, bn1_b, bn1_m, bn1_v, conv2_w, bn2_g, bn2_b,
               bn2_m, bn2_v, w_msg, b_msg, w_ih, b_ih, w_hh, b_hh, out):
    ctx = ExitStack()
    with ctx:
        def sb(name, shape, dt=F32):
            return ctx.enter_context(nc.sbuf_tensor(name, shape, dt))

        def sem(name):
            return ctx.enter_context(nc.semaphore(name))

        ident = sb("ident", [P, P])
        par = sb("par", [P, 24])
        se_b = sb("se_b", [SK, 1])
        wt_hi = sb("wt_hi", [P, NBLK, P], F32R)
        wt_lo = sb("wt_lo", [P, NBLK, P], F32R)
        bm_raw = sb("bm_raw", [33, P])
        bm_hi = sb("bm_hi", [33, P], F32R)
        bm = sb("bm", [33, CB, P], F32R)
        ones = sb("ones", [33, P], F32R)
        xin = sb("xin", [P, NCH, CB, P])
        xres = sb("xres", [P, NCH, CB, P])
        outb = sb("outb", [P, NCH, CB, P])
        stats = sb("stats", [P, GB, 6])
        mv = sb("mv", [P, GB, 2])
        vpe = sb("vpe", [P, GB])
        rstd = sb("rstd", [P, GB])
        neg_half = sb("neg_half", [P, GB])
        hn = sb("hn", [P, NCH, CB, P])
        hf = sb("hf", [P, GW])
        hf2 = sb("hf2", [P, GW])
        h_hi = sb("h_hi", [P, GW], F32R)
        h_lo = sb("h_lo", [P, GW], F32R)
        cp = sb("cp", [P, GB, CPAD])
        ua = sb("ua", [P, GB, UPAD])
        uc = sb("uc", [P, GB, UPAD])
        vt = sb("vt", [P, 6, GB, QUART + 1])
        v_hi = sb("v_hi", [P, 9, GB, VPAD], F32R)
        v_lo = sb("v_lo", [P, 9, GB, VPAD], F32R)
        mbs = sb("mbs", [P, GB, QUART])
        ma = sb("ma", [P, GB, HALF])
        mb = sb("mb", [P, GB, HALF])
        mc = sb("mc", [P, GB, HALF])
        xc_hi = sb("xc_hi", [P, GW], F32R)
        xc_lo = sb("xc_lo", [P, GW], F32R)
        left = sb("left", [SK, GB, P])
        right = sb("right", [SK, GB, P])
        m_hi = sb("m_hi", [P, GB, P], F32R)
        m_lo = sb("m_lo", [P, GB, P], F32R)
        at_hi = sb("at_hi", [P, GB, P], F32R)
        at_lo = sb("at_lo", [P, GB, P], F32R)
        n_hi = sb("n_hi", [P, GW], F32R)
        n_lo = sb("n_lo", [P, GW], F32R)
        scratch = sb("scratch", [P, 9216])
        spans = [0, 0]

        def cut(width, which):
            a = spans[which]
            spans[which] += width
            assert spans[which] <= 9216
            return scratch[:, a:a + width]

        w2 = cut(P * TAPS, 0).rearrange("p (c k) -> p c k", k=TAPS)
        f1 = {u: cut(LEN1[u] * P, 0).rearrange("p (k c) -> p k c", c=P) for u in ORDER}
        fs = {u: cut((LEN1[u] + 1) // 2 * P, 0).rearrange("p (k c) -> p k c", c=P) for u in ORDER}
        w1_raw, msg_raw, se_raw = cut(P, 0), cut(P, 0), cut(P, 0)
        ih_raw = cut(6 * P, 0).rearrange("p (g k c) -> p g k c", g=3, k=2)
        hh_raw = cut(3 * P, 0).rearrange("p (g c) -> p g c", g=3)
        mask = cut(GW, 1).rearrange("p (b m) -> p b m", m=P)
        aff = cut(GW, 1).rearrange("p (b m) -> p b m", m=P)
        y = cut(GW, 1)
        pa = cut(GB * HALF, 1).rearrange("p (b j) -> p b j", j=HALF)
        pc = cut(GB * HALF, 1).rearrange("p (b j) -> p b j", j=HALF)
        gn = [cut(CW, 1) for _ in range(NCH)]
        gr = [cut(CW, 1) for _ in range(NCH)]
        gz = [cut(CW, 1) for _ in range(NCH)]
        gw = [cut(CW, 1) for _ in range(NCH)]

        bank = [ctx.enter_context(nc.psum_tensor(f"bank{i}", [P, CW], F32)) for i in range(8)]

        w_landed, c2_landed, par_landed = sem("w_landed"), sem("c2_landed"), sem("par_landed")
        x_landed = [sem(f"x_landed{c}") for c in range(NCH)]
        xres_landed = [sem(f"xres_landed{c}") for c in range(NCH)]
        mask_landed = sem("mask_landed")
        out_stored = [sem(f"out_stored{c}") for c in range(NCH)]
        pool_set, pool_par, ident_ready = sem("pool_set"), sem("pool_par"), sem("ident_ready")
        dve_set, dve_w, wt_ps, wt_hi_ready, wt_lo_ready = (
            sem("dve_set"), sem("dve_w"), sem("wt_ps"), sem("wt_hi_ready"), sem("wt_lo_ready"))
        stats_ready, mv_ready, rstd_ready, vpe_ready, hn_ready = (
            sem("stats_ready"), sem("mv_ready"), sem("rstd_ready"), sem("vpe_ready"), sem("hn_ready"))
        ht_ps, hf_ready, h_hi_ready, h_lo_ready, hf2_ready = (
            sem("ht_ps"), sem("hf_ready"), sem("h_hi_ready"), sem("h_lo_ready"), sem("hf2_ready"))
        conv1_ps, c_ready, u_ready, t_ready, v_hi_ready, v_lob_ready, v_loac_ready = (
            sem("conv1_ps"), sem("c_ready"), sem("u_ready"), sem("t_ready"), sem("v_hi_ready"),
            sem("v_lob_ready"), sem("v_loac_ready"))
        conv2_ps, mbs_ready, m_ready, p_ready, y_ready, xc_hi_ready, xc_lo_ready = (
            sem("conv2_ps"), sem("mbs_ready"), sem("m_ready"), sem("p_ready"), sem("y_ready"),
            sem("xc_hi_ready"), sem("xc_lo_ready"))
        s_ps, s_ready, sq_ready, dist_ps, e_ready, a_ready = (
            sem("s_ps"), sem("s_ready"), sem("sq_ready"), sem("dist_ps"),
            sem("e_ready"), sem("a_ready"))
        at_ps, at_hi_ready, at_lo_ready, msg_ps, m_hi_ready, m_lo_ready = (
            sem("at_ps"), sem("at_hi_ready"), sem("at_lo_ready"), sem("msg_ps"), sem("m_hi_ready"),
            sem("m_lo_ready"))
        nmp_ps, n_hi_ready, n_lo_ready = sem("nmp_ps"), sem("n_hi_ready"), sem("n_lo_ready")
        ghn_ps, r_ps, gin_ps, z_ps, ghn_ready, r_ready, z_ready = (
            sem("ghn_ps"), sem("r_ps"), sem("gin_ps"), sem("z_ps"), sem("ghn_ready"), sem("r_ready"),
            sem("z_ready"))
        rg_ready, v_ready, cand_ready, diff_ready, zd_ready, o_ready, ot_ps, out_ready = (
            sem("rg_ready"), sem("v_ready"), sem("cand_ready"), sem("diff_ready"), sem("zd_ready"),
            sem("o_ready"), sem("ot_ps"), sem("out_ready"))

        x_v = x.rearrange("(k b) n d -> k n b d", b=CB)
        out_v = out.rearrange("(k b) n d -> k n b d", b=CB)
        adj_v = adj.rearrange("(g b) n m -> g n b m", b=GB)

        blocks = []
        for u in ORDER:
            n = LEN1[u]
            for v in ORDER:
                if v == "b":
                    blocks += [fs[u][:, i, :] for i in range((n + 1) // 2)]
                elif v == "a":
                    blocks += [f1[u][:, 2 * i, :] for i in range((n + 1) // 2)]
                else:
                    blocks += [f1[u][:, 2 * i + 1, :] for i in range(n // 2)]
        blocks += [w1_raw, msg_raw] + [ih_raw[:, g, k, :] for g in range(3) for k in range(2)]
        blocks += [hh_raw[:, g, :] for g in range(3)] + [se_raw]
        assert len(blocks) == NBLK
        lots = [list(range(i, min(i + CB, NBLK))) for i in range(NT, NBLK, CB)]
        lots += [list(range(i, min(i + CB, NT))) for i in range(0, NT, CB)]
        plain = -(-(NBLK - NT) // CB)

        def vec(a):
            return a.rearrange("(p a) -> p a", a=1)

        def v_src(q):
            u, v = ORDER[q // 3], ORDER[q % 3]
            if v != "b":
                return vt[:, 2 * (q // 3) + (v == "c"), :, :]
            return u_view(u, -1, 1 + QUART, 1)

        def u_view(u, first, count, phase):
            if u == "b":
                a = 2 * (2 * first + phase) + 1 + 4
                return cp[:, :, a:a + 4 * (count - 1) + 1:4]
            a = 2 * first + phase + 2
            return (ua if u == "a" else uc)[:, :, a:a + 2 * (count - 1) + 1:2]

        block = ctx.enter_context(nc.Block())

        @block.sync
        def _(sp):
            def load_x(g, c):
                sp.dma_start(xin[:, c], x_v[NCH * g + c]).then_inc(x_landed[c], 16)

            def load_mask(g):
                sp.dma_start(mask, adj_v[g]).then_inc(mask_landed, 16)

            for c in range(NCH):
                load_x(0, c)
            sp.dma_start(w2, conv2_w).then_inc(c2_landed, 16)
            for i, p in enumerate((bn1_g, bn1_b, bn1_m, bn1_v, bn2_g, bn2_b, bn2_m, bn2_v)):
                sp.dma_start(par[:, i:i + 1], vec(p)).then_inc(par_landed, 16)
            for i in range(3):
                sp.dma_start(par[:, BIR + i:BIR + i + 1], vec(b_ih[i * P:(i + 1) * P])).then_inc(par_landed, 16)
                sp.dma_start(par[:, BHR + i:BHR + i + 1], vec(b_hh[i * P:(i + 1) * P])).then_inc(par_landed, 16)
            sp.wait_ge(pool_set, 3)
            for r in S_ROWS:
                sp.dma_start(se_raw[r:r + 3, :], w_se).then_inc(w_landed, 16)
                sp.dma_start(se_b[r:r + 3, :], vec(b_se)).then_inc(w_landed, 16)
            for r in (0, 32):
                sp.dma_start(bm_raw[r:r + 1, :], b_msg.rearrange("(a d) -> a d", a=1)).then_inc(w_landed, 16)
            sp.wait_ge(wt_lo_ready, len(lots))
            load_mask(0)

            def body(g, ahead):
                for c in range(NCH):
                    previous(sp, out_ready, NCH * g)
                    sp.dma_start(xres[:, c], x_v[NCH * g + c]).then_inc(xres_landed[c], 16)
                if ahead:
                    sp.wait_ge(hn_ready, NCH * g + NCH)
                    for c in range(NCH):
                        load_x(g + 1, c)
                    sp.wait_ge(a_ready, NCH * g + NCH)
                    load_mask(g + 1)
                for c in range(NCH):
                    sp.wait_ge(out_ready, NCH * g + c + 1)
                    sp.dma_start(out_v[NCH * g + c], outb[:, c]).then_inc(out_stored[c], 16)

            body(0, True)
            with sp.Fori(1, NG - 1) as g:
                body(g, True)
            body(NG - 1, False)
            for c in range(NCH):
                sp.wait_ge(out_stored[c], 16 * NG)

        @block.gpsimd
        def _(pool):
            pool.memset(se_raw, 0.0).then_inc(pool_set, 1)
            pool.memset(se_b[:], 0.0).then_inc(pool_set, 1)
            pool.memset(bm_raw[:], 0.0).then_inc(pool_set, 1)
            pool.memset(ident[:], 0.0).then_inc(pool_set, 1)
            pool.memset(neg_half[:], -0.5).then_inc(pool_set, 1)
            pool.wait_ge(pool_set, 5)
            pool.affine_select(out=ident[:], in_=ident[:], compare_op=ALU.not_equal, fill=1.0, base=0,
                               pattern=[[-1, P]], channel_multiplier=1).then_inc(ident_ready, 1)

            def ln_scale(n):
                pool.wait_ge(vpe_ready, n)
                pool.tensor_tensor(rstd[:], vpe[:], neg_half[:], ALU.pow).then_inc(rstd_ready, 1)

            ln_scale(1)
            pool.wait_ge(par_landed, 14 * 16)
            for n, (g_, b_, m_, v_, sc, cb, t) in enumerate(((G1, B1, M1, V1, SC1, C1B, T1),
                                                             (G2, B2, M2, V2, SC2, C2B, T2))):
                col = lambda i: par[:, i:i + 1]
                pool.tensor_scalar(col(t), col(v_), EPS, None, ALU.add).then_inc(pool_par, 1)
                pool.wait_ge(pool_par, 5 * n + 1)
                pool.tensor_tensor(col(sc), col(t), neg_half[:, 0:1], ALU.pow).then_inc(pool_par, 1)
                pool.wait_ge(pool_par, 5 * n + 2)
                pool.tensor_tensor(col(sc), col(sc), col(g_), ALU.mult).then_inc(pool_par, 1)
                pool.wait_ge(pool_par, 5 * n + 3)
                pool.tensor_tensor(col(cb), col(m_), col(sc), ALU.mult).then_inc(pool_par, 1)
                pool.wait_ge(pool_par, 5 * n + 4)
                pool.tensor_tensor(col(cb), col(b_), col(cb), ALU.subtract).then_inc(pool_par, 1)

            def level1(g):
                pool.wait_ge(c_ready, NCH * g + NCH)
                previous(pool, t_ready, 6 * g)
                previous(pool, v_hi_ready, 9 * g)
                n = UPAD - 1
                pool.tensor_tensor(ua[:, :, 0:n], cp[:, :, 0:2 * n:2], cp[:, :, 1:2 * n:2],
                                   ALU.subtract).then_inc(u_ready, 1)
                pool.tensor_tensor(uc[:, :, 0:n], cp[:, :, 2:2 * n + 2:2], cp[:, :, 1:2 * n:2],
                                   ALU.subtract).then_inc(u_ready, 1)

            def body(g, ahead):
                level1(g)
                for c in range(NCH):
                    cs = slice(c * CB, (c + 1) * CB)
                    pool.wait_ge(e_ready, NCH * g + c + 1)
                    if c == 0:
                        pool.wait_ge(mask_landed, 16 * g + 16)
                    pool.tensor_tensor(aff[:, cs, :], aff[:, cs, :], mask[:, cs, :],
                                       ALU.mult).then_inc(a_ready, 1)
                for q in range(3, 9):
                    pool.wait_ge(v_hi_ready, 9 * g + q + 1)
                    pool.tensor_tensor(v_lo[:, q, :, 1:QUART + 2], v_src(q), v_hi[:, q, :, 1:QUART + 2],
                                       ALU.subtract).then_inc(v_loac_ready, 1)
                pool.wait_ge(m_ready, 6 * g + 2)
                hv = hf[:].rearrange("p (b j t) -> p b j t", j=HALF, t=2)
                previous(pool, y_ready, 2 * g)
                pool.tensor_tensor(pa, hv[:, :, :, 0], mb[:], ALU.add).then_inc(p_ready, 1)
                pool.tensor_tensor(pc, hv[:, :, :, 1], mb[:], ALU.add).then_inc(p_ready, 1)
                if ahead:
                    ln_scale(g + 2)
                for c in range(NCH):
                    pool.wait_ge(cand_ready, NCH * g + c + 1)
                    previous(pool, ot_ps, NCH * g)
                    pool.tensor_tensor(gw[c], hf2[:, c * CW:(c + 1) * CW], gn[c],
                                       ALU.subtract).then_inc(diff_ready, 1)

            body(0, True)
            with pool.Fori(1, NG - 1) as g:
                body(g, True)
            body(NG - 1, False)

        @block.scalar
        def _(act):
            act.dma_start(w1_raw, conv1_w.rearrange("o c k -> o (c k)")).then_inc(w_landed, 16)
            act.dma_start(msg_raw, w_msg).then_inc(w_landed, 16)
            act.dma_start(ih_raw, w_ih.rearrange("(g p) (k c) -> p g k c", g=3, k=2)).then_inc(w_landed, 16)
            act.dma_start(hh_raw, w_hh.rearrange("(g p) c -> p g c", g=3)).then_inc(w_landed, 16)

            def h_rows(g, c, first=False):
                cs = slice(c * CW, (c + 1) * CW)
                act.wait_ge(ht_ps, NCH * g + c + 1)
                if not first:
                    previous(act, hf2_ready, g)
                    previous(act, p_ready, 2 * g)
                act.activation(hf[:, cs], bank[c][:], ACT.Relu).then_inc(hf_ready, 1)
                act.activation(h_hi[:, cs], bank[c][:], ACT.Relu).then_inc(h_hi_ready, 1)

            for n, lot in enumerate(lots):
                if n == plain:
                    for c in range(NCH):
                        h_rows(0, c, first=True)
                act.wait_ge(wt_ps, n + 1)
                w = len(lot)
                act.activation(wt_hi[:, lot[0]:lot[0] + w, :], bank[2 + n % 6][:, 0:w * P],
                               ACT.Copy).then_inc(wt_hi_ready, 1)
            act.wait_ge(dve_set, 15)
            act.wait_ge(pool_par, 10)
            act.wait_ge(w_landed, 12 * 16)

            def v_high(g, q):
                u, v = ORDER[q // 3], ORDER[q % 3]
                if v != "b":
                    act.wait_ge(t_ready, 6 * g + 2 * (q // 3) + (v == "c") + 1)
                elif u != "b":
                    act.wait_ge(u_ready, 2 * g + "ac".index(u) + 1)
                else:
                    act.wait_ge(c_ready, NCH * g + NCH)
                previous(act, conv2_ps, 9 * g)
                act.activation(v_hi[:, q, :, 1:QUART + 2], v_src(q), ACT.Copy).then_inc(v_hi_ready, 1)

            def m_shared(g, u):
                act.wait_ge(conv2_ps, 9 * g + 3 * u + 1)
                previous(act, m_ready, 6 * g + 2 * u)
                src = bank[0][:, 0:GB * QUART].rearrange("p (b l) -> p b l", l=QUART)
                if u == 0:
                    act.activation(mbs[:], src, ACT.Identity, bias=par[:, C2B:C2B + 1]).then_inc(mbs_ready, 1)
                else:
                    act.activation(mbs[:], src, ACT.Copy).then_inc(mbs_ready, 1)

            def at_high(g, c):
                act.wait_ge(at_ps, NCH * g + c + 1)
                act.activation(at_hi[:, c * CB:(c + 1) * CB, :], bank[3][:], ACT.Copy).then_inc(at_hi_ready, 1)

            def n_high(g, c):
                act.wait_ge(nmp_ps, NCH * g + c + 1)
                act.activation(n_hi[:, c * CW:(c + 1) * CW], bank[6 + c][:], ACT.Copy).then_inc(n_hi_ready, 1)

            def body(g, ahead):
                for c in range(NCH):
                    act.wait_ge(conv1_ps, NCH * g + c + 1)
                    previous(act, u_ready, 2 * g)
                    previous(act, v_lob_ready, 3 * g)
                    act.activation(cp[:, c * CB:(c + 1) * CB, 4:4 + P],
                                   bank[2 + c][:].rearrange("p (b n) -> p b n", n=P), ACT.Relu,
                                   bias=par[:, C1B:C1B + 1]).then_inc(c_ready, 1)
                for c in range(NCH):
                    cs = slice(c * CB, (c + 1) * CB)
                    act.wait_ge(s_ps, NCH * g + c + 1)
                    for dst, r in ((right, 32), (left, 64)):
                        act.activation(dst[r:r + 3, cs, :], bank[4 + c][r:r + 3, :], ACT.Square,
                                       bias=se_b[r:r + 3, 0:1]).then_inc(sq_ready, 1)
                for q in range(3):
                    v_high(g, q)
                previous(act, diff_ready, NCH * g)
                act.activation(hf2[:], hf[:], ACT.Copy).then_inc(hf2_ready, 1)
                for c in range(NCH):
                    act.wait_ge(msg_ps, NCH * g + c + 1)
                    act.activation(m_hi[:, c * CB:(c + 1) * CB, :], bank[6 + c][:], ACT.Relu).then_inc(m_hi_ready, 1)
                for c in range(NCH):
                    act.wait_ge(dist_ps, NCH * g + c + 1)
                    act.activation(aff[:, c * CB:(c + 1) * CB, :], bank[4 + c][:], ACT.Exp,
                                   scale=2.0).then_inc(e_ready, 1)
                for q in range(3, 6):
                    v_high(g, q)
                m_shared(g, 0)
                for q in range(6, 9):
                    v_high(g, q)
                at_high(g, 0)
                m_shared(g, 1)
                at_high(g, 1)
                n_high(g, 0)
                n_high(g, 1)
                m_shared(g, 2)
                for c in range(NCH):
                    act.wait_ge(y_ready, 2 * g + 2)
                    cs = slice(c * CW, (c + 1) * CW)
                    act.activation(xc_hi[:, cs], y[:, cs], ACT.Relu).then_inc(xc_hi_ready, 1)
                for c in range(NCH):
                    previous(act, o_ready, NCH * g)
                    act.wait_ge(ghn_ps, NCH * g + c + 1)
                    act.activation(gn[c], bank[3][:], ACT.Identity, bias=par[:, HN:HN + 1],
                                   scale=0.5).then_inc(ghn_ready, 1)
                    act.wait_ge(r_ps, NCH * g + c + 1)
                    act.activation(gr[c], bank[4][:], ACT.Tanh, bias=par[:, HR:HR + 1],
                                   scale=0.5).then_inc(r_ready, 1)
                    act.wait_ge(v_ready, NCH * g + c + 1)
                    act.activation(gn[c], gn[c], ACT.Tanh, bias=par[:, BIN:BIN + 1]).then_inc(cand_ready, 1)
                    act.wait_ge(z_ps, NCH * g + c + 1)
                    act.activation(gz[c], bank[6][:], ACT.Tanh, bias=par[:, HZ:HZ + 1],
                                   scale=0.5).then_inc(z_ready, 1)
                if ahead:
                    for c in range(NCH):
                        h_rows(g + 1, c)

            body(0, True)
            with act.Fori(1, NG - 1) as g:
                body(g, True)
            body(NG - 1, False)

        @block.vector
        def _(dve):
            def ln_stats(g):
                for c in range(NCH):
                    dve.wait_ge(x_landed[c], 16 * g + 16)
                    for b in range(CB):
                        last = dve.bn_stats(stats[:, c * CB + b, :], xin[:, c, b, :])
                last.then_inc(stats_ready, 1)

            def ln_moments(g):
                for b in range(GB):
                    last = dve.bn_aggr(mv[:, b, :], stats[:, b, :])
                last.then_inc(mv_ready, 1)
                dve.wait_ge(mv_ready, g + 1)
                previous(dve, rstd_ready, g)
                dve.tensor_scalar(vpe[:], mv[:, :, 1], EPS, None, ALU.add).then_inc(vpe_ready, 1)

            def ln_rows(g):
                dve.wait_ge(rstd_ready, g + 1)
                previous(dve, ht_ps, NCH * g)
                for b in range(GB):
                    c, i = b // CB, b % CB
                    last = dve.tensor_scalar(hn[:, c, i, :], xin[:, c, i, :], mv[:, b, 0:1], rstd[:, b:b + 1],
                                             ALU.subtract, ALU.mult)
                    if i == CB - 1:
                        last.then_inc(hn_ready, 1)

            def h_low(g, c):
                cs = slice(c * CW, (c + 1) * CW)
                dve.wait_ge(h_hi_ready, NCH * g + c + 1)
                dve.tensor_tensor(h_lo[:, cs], hf[:, cs], h_hi[:, cs], ALU.subtract).then_inc(h_lo_ready, 1)

            dve.memset(cp[:], 0.0).then_inc(dve_set, 1)
            dve.memset(left[:], 0.0).then_inc(dve_set, 1)
            dve.memset(right[:], 0.0).then_inc(dve_set, 1)
            dve.memset(v_hi[:].bitcast(F32), 0.0).then_inc(dve_set, 1)
            dve.memset(v_lo[:].bitcast(F32), 0.0).then_inc(dve_set, 1)
            dve.memset(bm[:].bitcast(F32), 0.0).then_inc(dve_set, 1)
            dve.memset(ones[:].bitcast(F32), 1.0).then_inc(dve_set, 1)
            dve.wait_ge(dve_set, 7)
            dve.memset(left[32:35], -0.5).then_inc(dve_set, 1)
            dve.memset(right[64:67], -0.5).then_inc(dve_set, 1)
            ln_stats(0)
            dve.wait_ge(stats_ready, 1)
            ln_moments(0)
            ln_rows(0)
            dve.wait_ge(w_landed, 12 * 16)
            dve.tensor_copy(bm_hi[:], bm_raw[:]).then_inc(dve_set, 1)
            dve.wait_ge(dve_set, 10)
            for b in range(CB):
                dve.tensor_copy(bm[0:1, b, :], bm_raw[0:1, :])
                last = dve.tensor_tensor(bm[32:33, b, :], bm_raw[32:33, :], bm_hi[32:33, :], ALU.subtract)
            last.then_inc(dve_set, 1)
            dve.wait_ge(par_landed, 14 * 16)
            dve.tensor_tensor(par[:, HR:HR + 2], par[:, BIR:BIR + 2], par[:, BHR:BHR + 2],
                              ALU.add).then_inc(dve_set, 1)
            dve.tensor_scalar(par[:, HN:HN + 1], par[:, BHN:BHN + 1], 0.5, None, ALU.mult).then_inc(dve_set, 1)
            dve.wait_ge(dve_set, 13)
            dve.tensor_scalar(par[:, HR:HR + 2], par[:, HR:HR + 2], 0.5, None, ALU.mult).then_inc(dve_set, 1)
            dve.wait_ge(pool_par, 3)
            dve.tensor_scalar(w1_raw, w1_raw, par[:, SC1:SC1 + 1], None, ALU.mult).then_inc(dve_set, 1)
            dve.wait_ge(pool_par, 10)
            dve.wait_ge(c2_landed, 16)
            w2k = w2.rearrange("p c k -> p k c")
            dve.tensor_scalar(f1["a"], w2k[:, 0:TAPS:2, :], par[:, SC2:SC2 + 1], None, ALU.mult).then_inc(dve_w, 1)
            dve.tensor_scalar(f1["c"], w2k[:, 1:TAPS:2, :], par[:, SC2:SC2 + 1], None, ALU.mult).then_inc(dve_w, 1)
            dve.wait_ge(dve_w, 2)
            n = LEN1["c"]
            dve.tensor_tensor(f1["b"][:, 0:n, :], f1["a"][:, 0:n, :], f1["c"], ALU.add).then_inc(dve_w, 1)
            dve.tensor_copy(f1["b"][:, n:n + 1, :], f1["a"][:, n:n + 1, :]).then_inc(dve_w, 1)
            dve.wait_ge(dve_w, 4)
            for u in ORDER:
                n = LEN1[u]
                h = n // 2
                last = dve.tensor_tensor(fs[u][:, 0:h, :], f1[u][:, 0:2 * h:2, :], f1[u][:, 1:2 * h:2, :], ALU.add)
                if n % 2:
                    last = dve.tensor_copy(fs[u][:, h:h + 1, :], f1[u][:, n - 1:n, :])
            last.then_inc(dve_w, 1)
            for n, lot in enumerate(lots):
                if n == plain:
                    for c in range(NCH):
                        h_low(0, c)
                dve.wait_ge(wt_hi_ready, n + 1)
                w = len(lot)
                bs = slice(lot[0], lot[0] + w)
                dve.tensor_tensor(wt_lo[:, bs, :], bank[2 + n % 6][:, 0:w * P].rearrange("p (b c) -> p b c", c=P),
                                  wt_hi[:, bs, :], ALU.subtract).then_inc(wt_lo_ready, 1)

            def level2(g, u):
                name = ORDER[u]
                if name == "b":
                    dve.wait_ge(c_ready, NCH * g + NCH)
                else:
                    dve.wait_ge(u_ready, 2 * g + "ac".index(name) + 1)
                previous(dve, v_hi_ready, 9 * g)
                previous(dve, v_loac_ready, 6 * g)
                n = QUART + 1
                odd = u_view(name, -1, n, 1)
                dve.tensor_tensor(vt[:, 2 * u], u_view(name, -1, n, 0), odd, ALU.subtract).then_inc(t_ready, 1)
                dve.tensor_tensor(vt[:, 2 * u + 1], u_view(name, 0, n, 0), odd, ALU.subtract).then_inc(t_ready, 1)

            def join(g, u):
                dst = (mb, ma, mc)[u]
                dst = dst[:].rearrange("p b (l t) -> p b l t", t=2)
                dve.wait_ge(mbs_ready, 3 * g + u + 1)
                for t in range(2):
                    dve.wait_ge(conv2_ps, 9 * g + 3 * u + 2 + t)
                    if u == 0 and t == 0:
                        previous(dve, p_ready, 2 * g)
                    src = bank[1 + t][:, 0:GB * QUART].rearrange("p (b l) -> p b l", l=QUART)
                    dve.tensor_tensor(dst[:, :, :, t], src, mbs[:], ALU.add).then_inc(m_ready, 1)

            def join_y(g, t):
                dve.wait_ge(m_ready, 6 * g + 4 + 2 * t)
                dve.wait_ge(p_ready, 2 * g + t + 1)
                yv = y.rearrange("p (b j t) -> p b j t", j=HALF, t=2)
                dve.tensor_tensor(yv[:, :, :, t], (ma, mc)[t][:], (pa, pc)[t], ALU.add).then_inc(y_ready, 1)

            def body(g, ahead):
                level2(g, 0)
                for c in range(NCH):
                    dve.wait_ge(s_ps, NCH * g + c + 1)
                    for side in (left, right):
                        dve.tensor_scalar(side[0:3, c * CB:(c + 1) * CB, :],
                                          bank[4 + c][0:3, :].rearrange("p (b n) -> p b n", n=P),
                                          se_b[0:3, 0:1], None, ALU.add).then_inc(s_ready, 1)
                for q in range(3):
                    dve.wait_ge(v_hi_ready, 9 * g + q + 1)
                    dve.tensor_tensor(v_lo[:, q, :, 1:QUART + 2], v_src(q), v_hi[:, q, :, 1:QUART + 2],
                                      ALU.subtract).then_inc(v_lob_ready, 1)
                level2(g, 1)
                for c in range(NCH):
                    cs = slice(c * CB, (c + 1) * CB)
                    dve.wait_ge(m_hi_ready, NCH * g + c + 1)
                    dve.scalar_tensor_tensor(out=m_lo[:, cs, :], in0=bank[6 + c][:].rearrange("p (b n) -> p b n", n=P),
                                             scalar=0.0, in1=m_hi[:, cs, :], op0=ALU.max,
                                             op1=ALU.subtract).then_inc(m_lo_ready, 1)
                level2(g, 2)
                join(g, 0)
                for c in range(NCH):
                    cs = slice(c * CB, (c + 1) * CB)
                    dve.wait_ge(at_hi_ready, NCH * g + c + 1)
                    dve.tensor_tensor(at_lo[:, cs, :], bank[3][:].rearrange("p (b n) -> p b n", n=P),
                                      at_hi[:, cs, :], ALU.subtract).then_inc(at_lo_ready, 1)
                join(g, 1)
                join_y(g, 0)
                for c in range(NCH):
                    cs = slice(c * CW, (c + 1) * CW)
                    dve.wait_ge(n_hi_ready, NCH * g + c + 1)
                    dve.tensor_tensor(n_lo[:, cs], bank[6 + c][:], n_hi[:, cs], ALU.subtract).then_inc(n_lo_ready, 1)
                if ahead:
                    ln_stats(g + 1)
                    dve.wait_ge(stats_ready, g + 2)
                join(g, 2)
                join_y(g, 1)
                for c in range(NCH):
                    cs = slice(c * CW, (c + 1) * CW)
                    dve.wait_ge(xc_hi_ready, NCH * g + c + 1)
                    dve.scalar_tensor_tensor(out=xc_lo[:, cs], in0=y[:, cs], scalar=0.0, in1=xc_hi[:, cs],
                                             op0=ALU.max, op1=ALU.subtract).then_inc(xc_lo_ready, 1)
                if ahead:
                    ln_moments(g + 1)

                def reset(c):
                    dve.wait_ge(r_ready, NCH * g + c + 1)
                    dve.scalar_tensor_tensor(out=gn[c], in0=gr[c], scalar=1.0, in1=gn[c], op0=ALU.add,
                                             op1=ALU.mult).then_inc(rg_ready, 1)
                    dve.wait_ge(rg_ready, NCH * g + c + 1)
                    dve.wait_ge(gin_ps, NCH * g + c + 1)
                    dve.tensor_tensor(gn[c], bank[5][:], gn[c], ALU.add).then_inc(v_ready, 1)

                def update(c):
                    dve.wait_ge(z_ready, NCH * g + c + 1)
                    dve.wait_ge(diff_ready, NCH * g + c + 1)
                    dve.scalar_tensor_tensor(out=gw[c], in0=gz[c], scalar=1.0, in1=gw[c], op0=ALU.add,
                                             op1=ALU.mult).then_inc(zd_ready, 1)
                    dve.wait_ge(zd_ready, NCH * g + c + 1)
                    dve.scalar_tensor_tensor(out=gw[c], in0=gw[c], scalar=0.5, in1=gn[c], op0=ALU.mult,
                                             op1=ALU.add).then_inc(o_ready, 1)

                def residual(c):
                    dve.wait_ge(ot_ps, NCH * g + c + 1)
                    dve.wait_ge(xres_landed[c], 16 * g + 16)
                    previous(dve, out_stored[c], 16 * g)
                    dve.tensor_tensor(outb[:, c], bank[7][:].rearrange("p (b n) -> p b n", n=P), xres[:, c],
                                      ALU.add).then_inc(out_ready, 1)

                reset(0)
                if ahead:
                    ln_rows(g + 1)
                update(0)
                reset(1)
                residual(0)
                update(1)
                if ahead:
                    for c in range(NCH):
                        h_low(g + 1, c)
                residual(1)

            body(0, True)
            with dve.Fori(1, NG - 1) as g:
                body(g, True)
            body(NG - 1, False)

        @block.tensor
        def _(pe):
            def three(dst, blk, hi, lo, start, stop):
                pe.matmul(dst, wt_hi[:, blk, :], hi, start=start, stop=False)
                pe.matmul(dst, wt_hi[:, blk, :], lo, start=False, stop=False)
                return pe.matmul(dst, wt_lo[:, blk, :], hi, start=False, stop=stop)

            def h_transpose(g, c):
                pe.wait_ge(hn_ready, NCH * g + c + 1)
                for b in range(CB):
                    last = pe.transpose(bank[c][:, b * P:(b + 1) * P], hn[:, c, b, :], ident[:])
                last.then_inc(ht_ps, 1)

            pe.wait_ge(ident_ready, 1)
            pe.wait_ge(w_landed, 12 * 16)
            for n, lot in enumerate(lots):
                if n == 0:
                    pe.wait_ge(dve_set, 15)
                if n == plain:
                    for c in range(NCH):
                        h_transpose(0, c)
                    pe.wait_ge(dve_w, 5)
                if n >= 6:
                    previous(pe, wt_lo_ready, n - 5)
                for i, blk in enumerate(lot):
                    last = pe.transpose(bank[2 + n % 6][:, i * P:(i + 1) * P], blocks[blk], ident[:])
                last.then_inc(wt_ps, 1)
            pe.wait_ge(wt_lo_ready, len(lots))

            def sub_conv(g, q):
                at, n = SUBS[q]
                u, v = q // 3, q % 3
                if u == 0:
                    pe.wait_ge(v_lob_ready, 3 * g + q + 1)
                else:
                    pe.wait_ge(v_loac_ready, 6 * g + q - 2)
                    if v == 0:
                        previous(pe, mbs_ready, 3 * g + u)
                    else:
                        pe.wait_ge(m_ready, 6 * g + 2 * (u - 1) + v)
                dst = bank[v][:, 0:GB * QUART].rearrange("p (b l) -> p b l", l=QUART)
                for i in range(n):
                    last = three(dst, at + i, v_hi[:, q, :, i:i + QUART], v_lo[:, q, :, i:i + QUART],
                                 i == 0, i == n - 1)
                last.then_inc(conv2_ps, 1)

            def gates(g, c):
                cs = slice(c * CW, (c + 1) * CW)
                h = (h_hi[:, cs], h_lo[:, cs])
                nm = (n_hi[:, cs], n_lo[:, cs])
                xc = (xc_hi[:, cs], xc_lo[:, cs])
                pe.wait_ge(at_lo_ready, NCH * g + NCH) if c == 0 else previous(pe, ghn_ready, NCH * g + c)
                three(bank[3][:], HH(N), *h, True, True).then_inc(ghn_ps, 1)
                pe.wait_ge(e_ready, NCH * g + NCH) if c == 0 else previous(pe, r_ready, NCH * g + c)
                three(bank[4][:], HH(R), *h, True, False)
                pe.wait_ge(n_lo_ready, NCH * g + NCH)
                three(bank[4][:], IH(R, 1), *nm, False, False)
                if c:
                    previous(pe, v_ready, NCH * g + c)
                three(bank[5][:], IH(N, 1), *nm, True, False)
                if c:
                    previous(pe, z_ready, NCH * g + c)
                three(bank[6][:], HH(Z), *h, True, False)
                three(bank[6][:], IH(Z, 1), *nm, False, False)
                pe.wait_ge(xc_lo_ready, NCH * g + c + 1)
                three(bank[4][:], IH(R, 0), *xc, False, True).then_inc(r_ps, 1)
                three(bank[5][:], IH(N, 0), *xc, False, True).then_inc(gin_ps, 1)
                three(bank[6][:], IH(Z, 0), *xc, False, True).then_inc(z_ps, 1)

            def out_transpose(g, c):
                pe.wait_ge(o_ready, NCH * g + c + 1)
                if c:
                    previous(pe, out_ready, NCH * g + c)
                for b in range(CB):
                    last = pe.transpose(bank[7][:, b * P:(b + 1) * P], gw[c][:, b * P:(b + 1) * P], ident[:])
                last.then_inc(ot_ps, 1)

            def a_transpose(g, c):
                pe.wait_ge(a_ready, NCH * g + c + 1)
                pe.wait_ge(c_ready, NCH * g + NCH) if c == 0 else previous(pe, at_lo_ready, NCH * g + c)
                for b in range(CB):
                    last = pe.transpose(bank[3][:, b * P:(b + 1) * P], aff[:, c * CB + b, :], ident[:])
                last.then_inc(at_ps, 1)

            def gather(g, c):
                pe.wait_ge(m_lo_ready, NCH * g + c + 1)
                pe.wait_ge(at_lo_ready, NCH * g + c + 1)
                for b in range(CB):
                    i = c * CB + b
                    dst = bank[6 + c][:, b * P:(b + 1) * P]
                    pe.matmul(dst, m_hi[:, i, :], at_hi[:, i, :], start=True, stop=False)
                    pe.matmul(dst, m_hi[:, i, :], at_lo[:, i, :], start=False, stop=False)
                    last = pe.matmul(dst, m_lo[:, i, :], at_hi[:, i, :], start=False, stop=True)
                last.then_inc(nmp_ps, 1)

            def body(g, ahead):
                for c in range(NCH):
                    cs = slice(c * CW, (c + 1) * CW)
                    pe.wait_ge(h_lo_ready, NCH * g + c + 1)
                    previous(pe, m_ready, 6 * g) if c == 0 else previous(pe, ghn_ready, NCH * g)
                    three(bank[2 + c][:], CONV1, h_hi[:, cs], h_lo[:, cs], True, True).then_inc(conv1_ps, 1)
                for c in range(NCH):
                    cs = slice(c * CW, (c + 1) * CW)
                    previous(pe, r_ready, NCH * g) if c == 0 else previous(pe, v_ready, NCH * g)
                    dst = bank[4 + c][0:96, :]
                    pe.matmul(dst, wt_hi[:, SE, 0:96], h_hi[:, cs], start=True, stop=False)
                    pe.matmul(dst, wt_hi[:, SE, 0:96], h_lo[:, cs], start=False, stop=False)
                    pe.matmul(dst, wt_lo[:, SE, 0:96], h_hi[:, cs], start=False, stop=True).then_inc(s_ps, 1)
                for c in range(NCH):
                    previous(pe, z_ready, NCH * g) if c == 0 else previous(pe, out_ready, NCH * g)
                    pe.matmul(bank[6 + c][:], ones[:], bm[:], start=True, stop=False)
                    for b in range(CB):
                        hs = slice((c * CB + b) * P, (c * CB + b + 1) * P)
                        dst = bank[6 + c][:, b * P:(b + 1) * P]
                        pe.matmul(dst, h_hi[:, hs], wt_hi[:, MSG, :], start=False, stop=False)
                        pe.matmul(dst, h_hi[:, hs], wt_lo[:, MSG, :], start=False, stop=False)
                        last = pe.matmul(dst, h_lo[:, hs], wt_hi[:, MSG, :], start=False, stop=(b == CB - 1))
                    last.then_inc(msg_ps, 1)
                for c in range(NCH):
                    pe.wait_ge(s_ready, 2 * (NCH * g + c + 1))
                    pe.wait_ge(sq_ready, 2 * (NCH * g + c + 1))
                    for b in range(CB):
                        last = pe.matmul(bank[4 + c][:, b * P:(b + 1) * P], left[:, c * CB + b, :],
                                         right[:, c * CB + b, :], start=True, stop=True)
                    last.then_inc(dist_ps, 1)
                for q in range(9):
                    sub_conv(g, q)
                    if q in (2, 3):
                        a_transpose(g, q - 2)
                    if q in (4, 5):
                        gather(g, q - 4)
                gates(g, 0)
                gates(g, 1)
                out_transpose(g, 0)
                if ahead:
                    for c in range(NCH):
                        h_transpose(g + 1, c)
                out_transpose(g, 1)

            body(0, True)
            with pe.Fori(1, NG - 1) as g:
                body(g, True)
            body(NG - 1, False)


def previous(engine, semaphore, count):
    if not isinstance(count, int) or count > 0:
        engine.wait_ge(semaphore, count)


_INS = ["x", "adj", "w_se", "b_se", "conv1_w", "bn1_g", "bn1_b", "bn1_m", "bn1_v", "conv2_w", "bn2_g", "bn2_b",
        "bn2_m", "bn2_v", "w_msg", "b_msg", "w_ih", "b_ih", "w_hh", "b_hh"]


def kernel(**inputs):
    import numpy as np
    import concourse.bacc as bacc
    from concourse.bass_utils import run_bass_kernel_spmd

    nc = bacc.Bacc("TRN2", target_bir_lowering=False, num_devices=1)
    arrays, args = {}, []
    for name in _INS:
        a = np.ascontiguousarray(inputs[name if name in ("x", "adj") else "L0_gnn_" + name])
        arrays[f"in_{name}"] = a
        args.append(nc.dram_tensor(f"in_{name}", a.shape, mybir.dt.from_np(a.dtype), kind="ExternalInput").ap())
    out = nc.dram_tensor("out", (NB, P, P), F32, kind="ExternalOutput").ap()
    gnn_kernel(nc, *args, out)
    return run_bass_kernel_spmd(nc, [arrays], core_ids=[0]).results[0]["out"]
```

```python
from contextlib import ExitStack

import concourse.bass as bass
from concourse import mybir

F32 = mybir.dt.float32
F32R = mybir.dt.float32r
ALU = mybir.AluOpType
ACT = mybir.ActivationFunctionType

P = 128
NB = 64
GB = 8
CB = 4
NCH = GB // CB
NG = NB // GB
CW = CB * P
GW = GB * P
TAPS = 17
EPS = 1e-5

CPAD, UPAD, VPAD = P + 8, P // 2 + 4, P // 4 + 4
HALF, QUART = P // 2, P // 4
ORDER = "bac"
LEN1 = {"a": (TAPS + 1) // 2, "b": (TAPS + 1) // 2, "c": TAPS // 2}


def sub_taps():
    at, out = 0, []
    for u in ORDER:
        for v in ORDER:
            n = LEN1[u] // 2 if v == "c" else (LEN1[u] + 1) // 2
            out.append((at, n))
            at += n
    return out, at


SUBS, NT = sub_taps()
CONV1, MSG = NT, NT + 1
def IH(gate, part):
    return NT + 2 + 2 * gate + part
def HH(gate):
    return NT + 8 + gate
SE = NT + 11
NBLK = NT + 12
R, Z, N = 0, 1, 2
Z_BANK = (6, 2)
S_ROWS = (0, 32, 64)
SK = 67
(G1, B1, M1, V1, G2, B2, M2, V2, BIR, BIZ, BIN, BHR, BHZ, BHN,
 SC1, SC2, C1B, C2B, HR, HZ, HN, T1, T2) = range(23)


def gnn_kernel(nc, x, adj, w_se, b_se, conv1_w, bn1_g, bn1_b, bn1_m, bn1_v, conv2_w, bn2_g, bn2_b,
               bn2_m, bn2_v, w_msg, b_msg, w_ih, b_ih, w_hh, b_hh, out):
    ctx = ExitStack()
    with ctx:
        def sb(name, shape, dt=F32):
            return ctx.enter_context(nc.sbuf_tensor(name, shape, dt))

        def sem(name):
            return ctx.enter_context(nc.semaphore(name))

        ident = sb("ident", [P, P])
        par = sb("par", [P, 24])
        se_b = sb("se_b", [SK, 1])
        wt_hi = sb("wt_hi", [P, NBLK, P], F32R)
        wt_lo = sb("wt_lo", [P, NBLK, P], F32R)
        bm_raw = sb("bm_raw", [33, P])
        bm_hi = sb("bm_hi", [33, P], F32R)
        bm = sb("bm", [33, CB, P], F32R)
        ones = sb("ones", [33, P], F32R)
        xin = sb("xin", [P, NCH, CB, P])
        xres = sb("xres", [P, NCH, CB, P])
        outb = sb("outb", [P, NCH, CB, P])
        stats = sb("stats", [P, GB, 6])
        mv = sb("mv", [P, GB, 2])
        vpe = sb("vpe", [P, GB])
        rstd = sb("rstd", [P, GB])
        neg_half = sb("neg_half", [P, GB])
        hn = sb("hn", [P, NCH, CB, P])
        hf = sb("hf", [P, GW])
        hf2 = sb("hf2", [P, GW])
        h_hi = sb("h_hi", [P, GW], F32R)
        h_lo = sb("h_lo", [P, GW], F32R)
        cp = sb("cp", [P, GB, CPAD])
        ua = sb("ua", [P, GB, UPAD])
        uc = sb("uc", [P, GB, UPAD])
        vt = sb("vt", [P, 6, GB, QUART + 1])
        v_hi = sb("v_hi", [P, 9, GB, VPAD], F32R)
        v_lo = sb("v_lo", [P, 9, GB, VPAD], F32R)
        mbs = sb("mbs", [P, GB, QUART])
        ma = sb("ma", [P, GB, HALF])
        mb = sb("mb", [P, GB, HALF])
        mc = sb("mc", [P, GB, HALF])
        xc_hi = sb("xc_hi", [P, GW], F32R)
        xc_lo = sb("xc_lo", [P, GW], F32R)
        left = sb("left", [SK, GB, P])
        right = sb("right", [SK, GB, P])
        msg = sb("msg", [P, GB, P])
        aff_t = sb("aff_t", [P, GB, P])
        wt_msg = sb("wt_msg", [P, P])
        n_hi = sb("n_hi", [P, GW], F32R)
        n_lo = sb("n_lo", [P, GW], F32R)
        scratch = sb("scratch", [P, 9216])
        spans = [0, 0]

        def cut(width, which):
            a = spans[which]
            spans[which] += width
            assert spans[which] <= 9216
            return scratch[:, a:a + width]

        w2 = cut(P * TAPS, 0).rearrange("p (c k) -> p c k", k=TAPS)
        f1 = {u: cut(LEN1[u] * P, 0).rearrange("p (k c) -> p k c", c=P) for u in ORDER}
        fs = {u: cut((LEN1[u] + 1) // 2 * P, 0).rearrange("p (k c) -> p k c", c=P) for u in ORDER}
        w1_raw, msg_raw, se_raw = cut(P, 0), cut(P, 0), cut(P, 0)
        ih_raw = cut(6 * P, 0).rearrange("p (g k c) -> p g k c", g=3, k=2)
        hh_raw = cut(3 * P, 0).rearrange("p (g c) -> p g c", g=3)
        mask = cut(GW, 1).rearrange("p (b m) -> p b m", m=P)
        aff = cut(GW, 1).rearrange("p (b m) -> p b m", m=P)
        y = cut(GW, 1)
        pa = cut(GB * HALF, 1).rearrange("p (b j) -> p b j", j=HALF)
        pc = cut(GB * HALF, 1).rearrange("p (b j) -> p b j", j=HALF)
        gn = [cut(CW, 1) for _ in range(NCH)]
        gr = [cut(CW, 1) for _ in range(NCH)]
        gz = [cut(CW, 1) for _ in range(NCH)]
        gw = [cut(CW, 1) for _ in range(NCH)]

        bank = [ctx.enter_context(nc.psum_tensor(f"bank{i}", [P, CW], F32)) for i in range(8)]

        w_landed, c2_landed, par_landed = sem("w_landed"), sem("c2_landed"), sem("par_landed")
        x_landed = [sem(f"x_landed{c}") for c in range(NCH)]
        xres_landed = [sem(f"xres_landed{c}") for c in range(NCH)]
        mask_landed = sem("mask_landed")
        out_stored = [sem(f"out_stored{c}") for c in range(NCH)]
        pool_set, pool_par, ident_ready = sem("pool_set"), sem("pool_par"), sem("ident_ready")
        dve_set, dve_w, wt_ps, wt_hi_ready, wt_lo_ready = (
            sem("dve_set"), sem("dve_w"), sem("wt_ps"), sem("wt_hi_ready"), sem("wt_lo_ready"))
        stats_ready, mv_ready, rstd_ready, vpe_ready, hn_ready = (
            sem("stats_ready"), sem("mv_ready"), sem("rstd_ready"), sem("vpe_ready"), sem("hn_ready"))
        ht_ps, h_used, hf_ready, h_hi_ready, h_lo_ready, hf2_ready = (
            sem("ht_ps"), sem("h_used"), sem("hf_ready"), sem("h_hi_ready"), sem("h_lo_ready"), sem("hf2_ready"))
        conv1_ps, c_ready, u_ready, t_ready, v_hi_ready, v_lob_ready, v_loac_ready = (
            sem("conv1_ps"), sem("c_ready"), sem("u_ready"), sem("t_ready"), sem("v_hi_ready"),
            sem("v_lob_ready"), sem("v_loac_ready"))
        conv2_ps, mbs_ready, m_ready, p_ready, y_ready, xc_hi_ready, xc_lo_ready = (
            sem("conv2_ps"), sem("mbs_ready"), sem("m_ready"), sem("p_ready"), sem("y_ready"),
            sem("xc_hi_ready"), sem("xc_lo_ready"))
        s_ps, s_ready, sq_ready, dist_ps, e_ready, a_ready = (
            sem("s_ps"), sem("s_ready"), sem("sq_ready"), sem("dist_ps"),
            sem("e_ready"), sem("a_ready"))
        at_ps, at_ready, msg_ps, msg_ready = sem("at_ps"), sem("at_ready"), sem("msg_ps"), sem("msg_ready")
        nmp_ps, n_hi_ready, n_lo_ready = sem("nmp_ps"), sem("n_hi_ready"), sem("n_lo_ready")
        ghn_ps, r_ps, gin_ps, z_ps, ghn_ready, r_ready, z_ready = (
            sem("ghn_ps"), sem("r_ps"), sem("gin_ps"), sem("z_ps"), sem("ghn_ready"), sem("r_ready"),
            sem("z_ready"))
        rg_ready, v_ready, cand_ready, diff_ready, zd_ready, o_ready, ot_ps, out_ready = (
            sem("rg_ready"), sem("v_ready"), sem("cand_ready"), sem("diff_ready"), sem("zd_ready"),
            sem("o_ready"), sem("ot_ps"), sem("out_ready"))

        x_v = x.rearrange("(k b) n d -> k n b d", b=CB)
        out_v = out.rearrange("(k b) n d -> k n b d", b=CB)
        adj_v = adj.rearrange("(g b) n m -> g n b m", b=GB)

        blocks = []
        for u in ORDER:
            n = LEN1[u]
            for v in ORDER:
                if v == "b":
                    blocks += [fs[u][:, i, :] for i in range((n + 1) // 2)]
                elif v == "a":
                    blocks += [f1[u][:, 2 * i, :] for i in range((n + 1) // 2)]
                else:
                    blocks += [f1[u][:, 2 * i + 1, :] for i in range(n // 2)]
        blocks += [w1_raw, msg_raw] + [ih_raw[:, g, k, :] for g in range(3) for k in range(2)]
        blocks += [hh_raw[:, g, :] for g in range(3)] + [se_raw]
        assert len(blocks) == NBLK
        lots = [list(range(i, min(i + CB, NBLK))) for i in range(NT, NBLK, CB)]
        lots += [list(range(i, min(i + CB, NT))) for i in range(0, NT, CB)]
        plain = -(-(NBLK - NT) // CB)

        def vec(a):
            return a.rearrange("(p a) -> p a", a=1)

        def v_src(q):
            u, v = ORDER[q // 3], ORDER[q % 3]
            if v != "b":
                return vt[:, 2 * (q // 3) + (v == "c"), :, :]
            return u_view(u, -1, 1 + QUART, 1)

        def u_view(u, first, count, phase):
            if u == "b":
                a = 2 * (2 * first + phase) + 1 + 4
                return cp[:, :, a:a + 4 * (count - 1) + 1:4]
            a = 2 * first + phase + 2
            return (ua if u == "a" else uc)[:, :, a:a + 2 * (count - 1) + 1:2]

        block = ctx.enter_context(nc.Block())

        @block.sync
        def _(sp):
            def load_x(g, c):
                sp.dma_start(xin[:, c], x_v[NCH * g + c]).then_inc(x_landed[c], 16)

            def load_mask(g):
                sp.dma_start(mask, adj_v[g]).then_inc(mask_landed, 16)

            for c in range(NCH):
                load_x(0, c)
            sp.dma_start(w2, conv2_w).then_inc(c2_landed, 16)
            for i, p in enumerate((bn1_g, bn1_b, bn1_m, bn1_v, bn2_g, bn2_b, bn2_m, bn2_v)):
                sp.dma_start(par[:, i:i + 1], vec(p)).then_inc(par_landed, 16)
            for i in range(3):
                sp.dma_start(par[:, BIR + i:BIR + i + 1], vec(b_ih[i * P:(i + 1) * P])).then_inc(par_landed, 16)
                sp.dma_start(par[:, BHR + i:BHR + i + 1], vec(b_hh[i * P:(i + 1) * P])).then_inc(par_landed, 16)
            sp.wait_ge(pool_set, 3)
            for r in S_ROWS:
                sp.dma_start(se_raw[r:r + 3, :], w_se).then_inc(w_landed, 16)
                sp.dma_start(se_b[r:r + 3, :], vec(b_se)).then_inc(w_landed, 16)
            for r in (0, 32):
                sp.dma_start(bm_raw[r:r + 1, :], b_msg.rearrange("(a d) -> a d", a=1)).then_inc(w_landed, 16)
            sp.wait_ge(wt_lo_ready, len(lots))
            load_mask(0)

            sp.wait_ge(hn_ready, NCH)
            for c in range(NCH):
                load_x(1, c)

            def body(g, ahead, ahead2):
                for c in range(NCH):
                    previous(sp, out_ready, NCH * g)
                    sp.dma_start(xres[:, c], x_v[NCH * g + c]).then_inc(xres_landed[c], 16)
                if ahead:
                    sp.wait_ge(a_ready, NCH * g + NCH)
                    load_mask(g + 1)
                if ahead2:
                    sp.wait_ge(hn_ready, NCH * g + 2 * NCH)
                    for c in range(NCH):
                        load_x(g + 2, c)
                for c in range(NCH):
                    sp.wait_ge(out_ready, NCH * g + c + 1)
                    sp.dma_start(out_v[NCH * g + c], outb[:, c]).then_inc(out_stored[c], 16)

            body(0, True, True)
            with sp.Fori(1, NG - 2) as g:
                body(g, True, True)
            body(NG - 2, True, False)
            body(NG - 1, False, False)
            for c in range(NCH):
                sp.wait_ge(out_stored[c], 16 * NG)

        @block.gpsimd
        def _(pool):
            pool.memset(se_raw, 0.0).then_inc(pool_set, 1)
            pool.memset(se_b[:], 0.0).then_inc(pool_set, 1)
            pool.memset(bm_raw[:], 0.0).then_inc(pool_set, 1)
            pool.memset(ident[:], 0.0).then_inc(pool_set, 1)
            pool.memset(neg_half[:], -0.5).then_inc(pool_set, 1)
            pool.wait_ge(pool_set, 5)
            pool.affine_select(out=ident[:], in_=ident[:], compare_op=ALU.not_equal, fill=1.0, base=0,
                               pattern=[[-1, P]], channel_multiplier=1).then_inc(ident_ready, 1)

            def ln_scale(n):
                pool.wait_ge(vpe_ready, n)
                pool.tensor_tensor(rstd[:], vpe[:], neg_half[:], ALU.pow).then_inc(rstd_ready, 1)

            ln_scale(1)
            pool.wait_ge(par_landed, 14 * 16)
            for n, (g_, b_, m_, v_, sc, cb, t) in enumerate(((G1, B1, M1, V1, SC1, C1B, T1),
                                                             (G2, B2, M2, V2, SC2, C2B, T2))):
                col = lambda i: par[:, i:i + 1]
                pool.tensor_scalar(col(t), col(v_), EPS, None, ALU.add).then_inc(pool_par, 1)
                pool.wait_ge(pool_par, 5 * n + 1)
                pool.tensor_tensor(col(sc), col(t), neg_half[:, 0:1], ALU.pow).then_inc(pool_par, 1)
                pool.wait_ge(pool_par, 5 * n + 2)
                pool.tensor_tensor(col(sc), col(sc), col(g_), ALU.mult).then_inc(pool_par, 1)
                pool.wait_ge(pool_par, 5 * n + 3)
                pool.tensor_tensor(col(cb), col(m_), col(sc), ALU.mult).then_inc(pool_par, 1)
                pool.wait_ge(pool_par, 5 * n + 4)
                pool.tensor_tensor(col(cb), col(b_), col(cb), ALU.subtract).then_inc(pool_par, 1)

            def level1(g):
                pool.wait_ge(c_ready, NCH * g + NCH)
                previous(pool, t_ready, 6 * g)
                previous(pool, v_hi_ready, 9 * g)
                n = UPAD - 1
                pool.tensor_tensor(ua[:, :, 0:n], cp[:, :, 0:2 * n:2], cp[:, :, 1:2 * n:2],
                                   ALU.subtract).then_inc(u_ready, 1)
                pool.tensor_tensor(uc[:, :, 0:n], cp[:, :, 2:2 * n + 2:2], cp[:, :, 1:2 * n:2],
                                   ALU.subtract).then_inc(u_ready, 1)

            def v_low(g, q):
                pool.wait_ge(v_hi_ready, 9 * g + q + 1)
                pool.tensor_tensor(v_lo[:, q, :, 1:QUART + 2], v_src(q), v_hi[:, q, :, 1:QUART + 2],
                                   ALU.subtract).then_inc(v_loac_ready, 1)

            def body(g, ahead):
                level1(g)
                for q in range(3, 6):
                    v_low(g, q)
                for c in range(NCH):
                    cs = slice(c * CB, (c + 1) * CB)
                    pool.wait_ge(e_ready, NCH * g + c + 1)
                    if c == 0:
                        pool.wait_ge(mask_landed, 16 * g + 16)
                    pool.tensor_tensor(aff[:, cs, :], aff[:, cs, :], mask[:, cs, :],
                                       ALU.mult).then_inc(a_ready, 1)
                for q in range(6, 9):
                    v_low(g, q)
                if ahead:
                    ln_scale(g + 2)
                pool.wait_ge(m_ready, 6 * g + 2)
                hv = hf[:].rearrange("p (b j t) -> p b j t", j=HALF, t=2)
                previous(pool, y_ready, 2 * g)
                pool.tensor_tensor(pa, hv[:, :, :, 0], mb[:], ALU.add).then_inc(p_ready, 1)
                pool.tensor_tensor(pc, hv[:, :, :, 1], mb[:], ALU.add).then_inc(p_ready, 1)
                for c in range(NCH):
                    pool.wait_ge(cand_ready, NCH * g + c + 1)
                    previous(pool, ot_ps, NCH * g)
                    pool.tensor_tensor(gw[c], hf2[:, c * CW:(c + 1) * CW], gn[c],
                                       ALU.subtract).then_inc(diff_ready, 1)

            body(0, True)
            with pool.Fori(1, NG - 1) as g:
                body(g, True)
            body(NG - 1, False)

        @block.scalar
        def _(act):
            act.dma_start(w1_raw, conv1_w.rearrange("o c k -> o (c k)")).then_inc(w_landed, 16)
            act.dma_start(msg_raw, w_msg).then_inc(w_landed, 16)
            act.dma_start(ih_raw, w_ih.rearrange("(g p) (k c) -> p g k c", g=3, k=2)).then_inc(w_landed, 16)
            act.dma_start(hh_raw, w_hh.rearrange("(g p) c -> p g c", g=3)).then_inc(w_landed, 16)

            def h_rows(g, c, first=False):
                cs = slice(c * CW, (c + 1) * CW)
                act.wait_ge(ht_ps, NCH * g + c + 1)
                if not first:
                    previous(act, hf2_ready, g)
                    previous(act, p_ready, 2 * g)
                    act.wait_ge(msg_ps, NCH * g)
                    act.wait_ge(h_used, NCH * (g - 1) + c + 1)
                act.activation(hf[:, cs], bank[c][:], ACT.Relu).then_inc(hf_ready, 1)
                act.activation(h_hi[:, cs], bank[c][:], ACT.Relu).then_inc(h_hi_ready, 1)

            for n, lot in enumerate(lots):
                if n == plain:
                    for c in range(NCH):
                        h_rows(0, c, first=True)
                act.wait_ge(wt_ps, n + 1)
                w = len(lot)
                if MSG in lot:
                    a = (MSG - lot[0]) * P
                    act.activation(wt_msg[:], bank[2 + n % 6][:, a:a + P], ACT.Copy)
                act.activation(wt_hi[:, lot[0]:lot[0] + w, :], bank[2 + n % 6][:, 0:w * P],
                               ACT.Copy).then_inc(wt_hi_ready, 1)
            act.wait_ge(dve_set, 15)
            act.wait_ge(pool_par, 10)
            act.wait_ge(w_landed, 12 * 16)

            def v_high(g, q):
                u, v = ORDER[q // 3], ORDER[q % 3]
                if v != "b":
                    act.wait_ge(t_ready, 6 * g + 2 * (q // 3) + (v == "c") + 1)
                elif u != "b":
                    act.wait_ge(u_ready, 2 * g + "ac".index(u) + 1)
                else:
                    act.wait_ge(c_ready, NCH * g + NCH)
                previous(act, conv2_ps, 9 * g)
                act.activation(v_hi[:, q, :, 1:QUART + 2], v_src(q), ACT.Copy).then_inc(v_hi_ready, 1)

            def m_shared(g, u):
                act.wait_ge(conv2_ps, 9 * g + 3 * u + 1)
                previous(act, m_ready, 6 * g + 2 * u)
                src = bank[0][:, 0:GB * QUART].rearrange("p (b l) -> p b l", l=QUART)
                if u == 0:
                    act.activation(mbs[:], src, ACT.Identity, bias=par[:, C2B:C2B + 1]).then_inc(mbs_ready, 1)
                else:
                    act.activation(mbs[:], src, ACT.Copy).then_inc(mbs_ready, 1)

            def at_rows(g, c):
                act.wait_ge(at_ps, NCH * g + c + 1)
                act.activation(aff_t[:, c * CB:(c + 1) * CB, :], bank[3][:], ACT.Copy).then_inc(at_ready, 1)

            def n_high(g, c):
                act.wait_ge(nmp_ps, NCH * g + c + 1)
                act.activation(n_hi[:, c * CW:(c + 1) * CW], bank[6 + c][:], ACT.Copy).then_inc(n_hi_ready, 1)

            def squares(g, c):
                act.wait_ge(s_ps, NCH * g + c + 1)
                for dst, r in ((right, 32), (left, 64)):
                    act.activation(dst[r:r + 3, c * CB:(c + 1) * CB, :], bank[4 + c][r:r + 3, :], ACT.Square,
                                   bias=se_b[r:r + 3, 0:1]).then_inc(sq_ready, 1)

            def head(g):
                for c in range(NCH):
                    act.wait_ge(conv1_ps, NCH * g + c + 1)
                    previous(act, u_ready, 2 * g)
                    previous(act, v_lob_ready, 3 * g)
                    act.activation(cp[:, c * CB:(c + 1) * CB, 4:4 + P],
                                   bank[c][:].rearrange("p (b n) -> p b n", n=P), ACT.Relu,
                                   bias=par[:, C1B:C1B + 1]).then_inc(c_ready, 1)
                v_high(g, 0)
                squares(g, 0)
                v_high(g, 1)
                v_high(g, 2)
                squares(g, 1)

            def body(g, ahead):
                v_high(g, 3)
                for c in range(NCH):
                    act.wait_ge(msg_ps, NCH * g + c + 1)
                    act.activation(msg[:, c * CB:(c + 1) * CB, :], bank[Z_BANK[c]][:], ACT.Relu).then_inc(msg_ready, 1)
                m_shared(g, 0)
                v_high(g, 4)
                v_high(g, 5)
                previous(act, diff_ready, NCH * g)
                act.activation(hf2[:], hf[:], ACT.Copy).then_inc(hf2_ready, 1)
                for c in range(NCH):
                    act.wait_ge(dist_ps, NCH * g + c + 1)
                    act.activation(aff[:, c * CB:(c + 1) * CB, :], bank[4 + c][:], ACT.Exp,
                                   scale=2.0).then_inc(e_ready, 1)
                for q in range(6, 9):
                    v_high(g, q)
                m_shared(g, 1)
                at_rows(g, 0)
                at_rows(g, 1)
                m_shared(g, 2)
                n_high(g, 0)
                n_high(g, 1)
                for c in range(NCH):
                    act.wait_ge(y_ready, 2 * g + 2)
                    cs = slice(c * CW, (c + 1) * CW)
                    act.activation(xc_hi[:, cs], y[:, cs], ACT.Relu).then_inc(xc_hi_ready, 1)
                for c in range(NCH):
                    previous(act, o_ready, NCH * g)
                    act.wait_ge(ghn_ps, NCH * g + c + 1)
                    act.activation(gn[c], bank[3][:], ACT.Identity, bias=par[:, HN:HN + 1],
                                   scale=0.5).then_inc(ghn_ready, 1)
                    if ahead:
                        h_rows(g + 1, c)
                    act.wait_ge(r_ps, NCH * g + c + 1)
                    act.activation(gr[c], bank[4][:], ACT.Tanh, bias=par[:, HR:HR + 1],
                                   scale=0.5).then_inc(r_ready, 1)
                    act.wait_ge(v_ready, NCH * g + c + 1)
                    act.activation(gn[c], gn[c], ACT.Tanh, bias=par[:, BIN:BIN + 1]).then_inc(cand_ready, 1)
                    act.wait_ge(z_ps, NCH * g + c + 1)
                    act.activation(gz[c], bank[Z_BANK[c]][:], ACT.Tanh, bias=par[:, HZ:HZ + 1],
                                   scale=0.5).then_inc(z_ready, 1)
                if ahead:
                    head(g + 1)

            head(0)
            body(0, True)
            with act.Fori(1, NG - 1) as g:
                body(g, True)
            body(NG - 1, False)

        @block.vector
        def _(dve):
            def ln_stats(g):
                for c in range(NCH):
                    dve.wait_ge(x_landed[c], 16 * g + 16)
                    for b in range(CB):
                        last = dve.bn_stats(stats[:, c * CB + b, :], xin[:, c, b, :])
                last.then_inc(stats_ready, 1)

            def ln_moments(g):
                for b in range(GB):
                    last = dve.bn_aggr(mv[:, b, :], stats[:, b, :])
                last.then_inc(mv_ready, 1)
                dve.wait_ge(mv_ready, g + 1)
                previous(dve, rstd_ready, g)
                dve.tensor_scalar(vpe[:], mv[:, :, 1], EPS, None, ALU.add).then_inc(vpe_ready, 1)

            def ln_rows(g):
                dve.wait_ge(rstd_ready, g + 1)
                previous(dve, ht_ps, NCH * g)
                for b in range(GB):
                    c, i = b // CB, b % CB
                    last = dve.tensor_scalar(hn[:, c, i, :], xin[:, c, i, :], mv[:, b, 0:1], rstd[:, b:b + 1],
                                             ALU.subtract, ALU.mult)
                    if i == CB - 1:
                        last.then_inc(hn_ready, 1)

            def h_low(g, c):
                cs = slice(c * CW, (c + 1) * CW)
                dve.wait_ge(h_hi_ready, NCH * g + c + 1)
                dve.tensor_tensor(h_lo[:, cs], hf[:, cs], h_hi[:, cs], ALU.subtract).then_inc(h_lo_ready, 1)

            dve.memset(cp[:], 0.0).then_inc(dve_set, 1)
            dve.memset(left[:], 0.0).then_inc(dve_set, 1)
            dve.memset(right[:], 0.0).then_inc(dve_set, 1)
            dve.memset(v_hi[:].bitcast(F32), 0.0).then_inc(dve_set, 1)
            dve.memset(v_lo[:].bitcast(F32), 0.0).then_inc(dve_set, 1)
            dve.memset(bm[:].bitcast(F32), 0.0).then_inc(dve_set, 1)
            dve.memset(ones[:].bitcast(F32), 1.0).then_inc(dve_set, 1)
            dve.wait_ge(dve_set, 7)
            dve.memset(left[32:35], -0.5).then_inc(dve_set, 1)
            dve.memset(right[64:67], -0.5).then_inc(dve_set, 1)
            ln_stats(0)
            dve.wait_ge(stats_ready, 1)
            ln_moments(0)
            ln_rows(0)
            dve.wait_ge(w_landed, 12 * 16)
            dve.tensor_copy(bm_hi[:], bm_raw[:]).then_inc(dve_set, 1)
            dve.wait_ge(dve_set, 10)
            for b in range(CB):
                dve.tensor_copy(bm[0:1, b, :], bm_raw[0:1, :])
                last = dve.tensor_tensor(bm[32:33, b, :], bm_raw[32:33, :], bm_hi[32:33, :], ALU.subtract)
            last.then_inc(dve_set, 1)
            dve.wait_ge(par_landed, 14 * 16)
            dve.tensor_tensor(par[:, HR:HR + 2], par[:, BIR:BIR + 2], par[:, BHR:BHR + 2],
                              ALU.add).then_inc(dve_set, 1)
            dve.tensor_scalar(par[:, HN:HN + 1], par[:, BHN:BHN + 1], 0.5, None, ALU.mult).then_inc(dve_set, 1)
            dve.wait_ge(dve_set, 13)
            dve.tensor_scalar(par[:, HR:HR + 2], par[:, HR:HR + 2], 0.5, None, ALU.mult).then_inc(dve_set, 1)
            dve.wait_ge(pool_par, 3)
            dve.tensor_scalar(w1_raw, w1_raw, par[:, SC1:SC1 + 1], None, ALU.mult).then_inc(dve_set, 1)
            dve.wait_ge(pool_par, 10)
            dve.wait_ge(c2_landed, 16)
            w2k = w2.rearrange("p c k -> p k c")
            dve.tensor_scalar(f1["a"], w2k[:, 0:TAPS:2, :], par[:, SC2:SC2 + 1], None, ALU.mult).then_inc(dve_w, 1)
            dve.tensor_scalar(f1["c"], w2k[:, 1:TAPS:2, :], par[:, SC2:SC2 + 1], None, ALU.mult).then_inc(dve_w, 1)
            dve.wait_ge(dve_w, 2)
            n = LEN1["c"]
            dve.tensor_tensor(f1["b"][:, 0:n, :], f1["a"][:, 0:n, :], f1["c"], ALU.add).then_inc(dve_w, 1)
            dve.tensor_copy(f1["b"][:, n:n + 1, :], f1["a"][:, n:n + 1, :]).then_inc(dve_w, 1)
            dve.wait_ge(dve_w, 4)
            for u in ORDER:
                n = LEN1[u]
                h = n // 2
                last = dve.tensor_tensor(fs[u][:, 0:h, :], f1[u][:, 0:2 * h:2, :], f1[u][:, 1:2 * h:2, :], ALU.add)
                if n % 2:
                    last = dve.tensor_copy(fs[u][:, h:h + 1, :], f1[u][:, n - 1:n, :])
            last.then_inc(dve_w, 1)
            for n, lot in enumerate(lots):
                if n == plain:
                    for c in range(NCH):
                        h_low(0, c)
                dve.wait_ge(wt_hi_ready, n + 1)
                w = len(lot)
                bs = slice(lot[0], lot[0] + w)
                dve.tensor_tensor(wt_lo[:, bs, :], bank[2 + n % 6][:, 0:w * P].rearrange("p (b c) -> p b c", c=P),
                                  wt_hi[:, bs, :], ALU.subtract).then_inc(wt_lo_ready, 1)

            def level2(g, u):
                name = ORDER[u]
                if name == "b":
                    dve.wait_ge(c_ready, NCH * g + NCH)
                else:
                    dve.wait_ge(u_ready, 2 * g + "ac".index(name) + 1)
                previous(dve, v_hi_ready, 9 * g)
                previous(dve, v_loac_ready, 6 * g)
                n = QUART + 1
                odd = u_view(name, -1, n, 1)
                dve.tensor_tensor(vt[:, 2 * u], u_view(name, -1, n, 0), odd, ALU.subtract).then_inc(t_ready, 1)
                dve.tensor_tensor(vt[:, 2 * u + 1], u_view(name, 0, n, 0), odd, ALU.subtract).then_inc(t_ready, 1)

            def join(g, u):
                dst = (mb, ma, mc)[u]
                dst = dst[:].rearrange("p b (l t) -> p b l t", t=2)
                dve.wait_ge(mbs_ready, 3 * g + u + 1)
                for t in range(2):
                    dve.wait_ge(conv2_ps, 9 * g + 3 * u + 2 + t)
                    if u == 0 and t == 0:
                        previous(dve, p_ready, 2 * g)
                    src = bank[1 + t][:, 0:GB * QUART].rearrange("p (b l) -> p b l", l=QUART)
                    dve.tensor_tensor(dst[:, :, :, t], src, mbs[:], ALU.add).then_inc(m_ready, 1)

            def join_y(g, t):
                dve.wait_ge(m_ready, 6 * g + 4 + 2 * t)
                dve.wait_ge(p_ready, 2 * g + t + 1)
                yv = y.rearrange("p (b j t) -> p b j t", j=HALF, t=2)
                dve.tensor_tensor(yv[:, :, :, t], (ma, mc)[t][:], (pa, pc)[t], ALU.add).then_inc(y_ready, 1)

            def side_rows(g, c):
                dve.wait_ge(s_ps, NCH * g + c + 1)
                for side in (left, right):
                    dve.tensor_scalar(side[0:3, c * CB:(c + 1) * CB, :],
                                      bank[4 + c][0:3, :].rearrange("p (b n) -> p b n", n=P),
                                      se_b[0:3, 0:1], None, ALU.add).then_inc(s_ready, 1)

            def v_low(g, q):
                dve.wait_ge(v_hi_ready, 9 * g + q + 1)
                dve.tensor_tensor(v_lo[:, q, :, 1:QUART + 2], v_src(q), v_hi[:, q, :, 1:QUART + 2],
                                  ALU.subtract).then_inc(v_lob_ready, 1)

            def head(g):
                level2(g, 0)
                v_low(g, 0)
                side_rows(g, 0)
                v_low(g, 1)
                v_low(g, 2)
                side_rows(g, 1)

            def body(g, ahead):
                def n_low(c):
                    cs = slice(c * CW, (c + 1) * CW)
                    dve.wait_ge(n_hi_ready, NCH * g + c + 1)
                    dve.tensor_tensor(n_lo[:, cs], bank[6 + c][:], n_hi[:, cs], ALU.subtract).then_inc(n_lo_ready, 1)

                level2(g, 1)
                level2(g, 2)
                if ahead:
                    ln_stats(g + 1)
                    dve.wait_ge(stats_ready, g + 2)
                join(g, 0)
                if ahead:
                    ln_moments(g + 1)
                join(g, 1)
                if ahead:
                    ln_rows(g + 1)
                join_y(g, 0)
                n_low(0)
                join(g, 2)
                join_y(g, 1)
                n_low(1)
                for c in range(NCH):
                    cs = slice(c * CW, (c + 1) * CW)
                    dve.wait_ge(xc_hi_ready, NCH * g + c + 1)
                    dve.scalar_tensor_tensor(out=xc_lo[:, cs], in0=y[:, cs], scalar=0.0, in1=xc_hi[:, cs],
                                             op0=ALU.max, op1=ALU.subtract).then_inc(xc_lo_ready, 1)
                def reset(c):
                    dve.wait_ge(r_ready, NCH * g + c + 1)
                    dve.scalar_tensor_tensor(out=gn[c], in0=gr[c], scalar=1.0, in1=gn[c], op0=ALU.add,
                                             op1=ALU.mult).then_inc(rg_ready, 1)
                    dve.wait_ge(rg_ready, NCH * g + c + 1)
                    dve.wait_ge(gin_ps, NCH * g + c + 1)
                    dve.tensor_tensor(gn[c], bank[5][:], gn[c], ALU.add).then_inc(v_ready, 1)

                def update(c):
                    dve.wait_ge(z_ready, NCH * g + c + 1)
                    dve.wait_ge(diff_ready, NCH * g + c + 1)
                    dve.scalar_tensor_tensor(out=gw[c], in0=gz[c], scalar=1.0, in1=gw[c], op0=ALU.add,
                                             op1=ALU.mult).then_inc(zd_ready, 1)
                    dve.wait_ge(zd_ready, NCH * g + c + 1)
                    dve.scalar_tensor_tensor(out=gw[c], in0=gw[c], scalar=0.5, in1=gn[c], op0=ALU.mult,
                                             op1=ALU.add).then_inc(o_ready, 1)

                def residual(c):
                    dve.wait_ge(ot_ps, NCH * g + c + 1)
                    dve.wait_ge(xres_landed[c], 16 * g + 16)
                    previous(dve, out_stored[c], 16 * g)
                    dve.tensor_tensor(outb[:, c], bank[7][:].rearrange("p (b n) -> p b n", n=P), xres[:, c],
                                      ALU.add).then_inc(out_ready, 1)

                if ahead:
                    h_low(g + 1, 0)
                reset(0)
                update(0)
                if ahead:
                    h_low(g + 1, 1)
                reset(1)
                residual(0)
                update(1)
                if ahead:
                    head(g + 1)
                residual(1)

            head(0)
            body(0, True)
            with dve.Fori(1, NG - 1) as g:
                body(g, True)
            body(NG - 1, False)

        @block.tensor
        def _(pe):
            def three(dst, blk, hi, lo, start, stop):
                pe.matmul(dst, wt_hi[:, blk, :], hi, start=start, stop=False)
                pe.matmul(dst, wt_hi[:, blk, :], lo, start=False, stop=False)
                return pe.matmul(dst, wt_lo[:, blk, :], hi, start=False, stop=stop)

            def h_transpose(g, c):
                pe.wait_ge(hn_ready, NCH * g + c + 1)
                previous(pe, mbs_ready, 3 * g) if c == 0 else previous(pe, m_ready, 6 * g)
                for b in range(CB):
                    last = pe.transpose(bank[c][:, b * P:(b + 1) * P], hn[:, c, b, :], ident[:])
                last.then_inc(ht_ps, 1)

            pe.wait_ge(ident_ready, 1)
            pe.wait_ge(w_landed, 12 * 16)
            for n, lot in enumerate(lots):
                if n == 0:
                    pe.wait_ge(dve_set, 15)
                if n == plain:
                    for c in range(NCH):
                        h_transpose(0, c)
                    pe.wait_ge(dve_w, 5)
                if n >= 6:
                    previous(pe, wt_lo_ready, n - 5)
                for i, blk in enumerate(lot):
                    last = pe.transpose(bank[2 + n % 6][:, i * P:(i + 1) * P], blocks[blk], ident[:])
                last.then_inc(wt_ps, 1)
            pe.wait_ge(wt_lo_ready, len(lots))

            def sub_conv(g, q):
                at, n = SUBS[q]
                u, v = q // 3, q % 3
                if u == 0:
                    pe.wait_ge(v_lob_ready, 3 * g + q + 1)
                    if v == 2:
                        pe.wait_ge(msg_ready, NCH * g + NCH)
                else:
                    pe.wait_ge(v_loac_ready, 6 * g + q - 2)
                    if v == 0:
                        previous(pe, mbs_ready, 3 * g + u)
                    else:
                        pe.wait_ge(m_ready, 6 * g + 2 * (u - 1) + v)
                dst = bank[v][:, 0:GB * QUART].rearrange("p (b l) -> p b l", l=QUART)
                for i in range(n):
                    last = three(dst, at + i, v_hi[:, q, :, i:i + QUART], v_lo[:, q, :, i:i + QUART],
                                 i == 0, i == n - 1)
                last.then_inc(conv2_ps, 1)

            def gates(g, c, ahead):
                cs = slice(c * CW, (c + 1) * CW)
                h = (h_hi[:, cs], h_lo[:, cs])
                nm = (n_hi[:, cs], n_lo[:, cs])
                xc = (xc_hi[:, cs], xc_lo[:, cs])
                pe.wait_ge(at_ready, NCH * g + NCH) if c == 0 else previous(pe, ghn_ready, NCH * g + c)
                three(bank[3][:], HH(N), *h, True, True).then_inc(ghn_ps, 1)
                pe.wait_ge(e_ready, NCH * g + NCH) if c == 0 else previous(pe, r_ready, NCH * g + c)
                three(bank[4][:], HH(R), *h, True, False)
                pe.wait_ge(m_ready, 6 * g + 6) if c else pe.wait_ge(n_lo_ready, NCH * g + 1)
                zb = bank[Z_BANK[c]][:]
                three(zb, HH(Z), *h, True, False).then_inc(h_used, 1)
                if ahead:
                    h_transpose(g + 1, c)
                pe.wait_ge(n_lo_ready, NCH * g + c + 1)
                three(bank[4][:], IH(R, 1), *nm, False, False)
                if c:
                    pe.wait_ge(v_ready, NCH * g + c)
                three(bank[5][:], IH(N, 1), *nm, True, False)
                three(zb, IH(Z, 1), *nm, False, False)
                pe.wait_ge(xc_lo_ready, NCH * g + c + 1)
                three(bank[4][:], IH(R, 0), *xc, False, True).then_inc(r_ps, 1)
                three(bank[5][:], IH(N, 0), *xc, False, True).then_inc(gin_ps, 1)
                three(zb, IH(Z, 0), *xc, False, True).then_inc(z_ps, 1)

            def out_transpose(g, c):
                pe.wait_ge(o_ready, NCH * g + c + 1)
                if c:
                    previous(pe, out_ready, NCH * g + c)
                for b in range(CB):
                    last = pe.transpose(bank[7][:, b * P:(b + 1) * P], gw[c][:, b * P:(b + 1) * P], ident[:])
                last.then_inc(ot_ps, 1)

            def a_transpose(g, c):
                pe.wait_ge(a_ready, NCH * g + c + 1)
                previous(pe, ghn_ready, NCH * g) if c == 0 else pe.wait_ge(at_ready, NCH * g + c)
                for b in range(CB):
                    last = pe.transpose(bank[3][:, b * P:(b + 1) * P], aff[:, c * CB + b, :], ident[:])
                last.then_inc(at_ps, 1)

            def gather(g, c):
                pe.wait_ge(msg_ready, NCH * g + c + 1)
                pe.wait_ge(at_ready, NCH * g + c + 1)
                if c:
                    previous(pe, out_ready, NCH * g)
                for b in range(CB):
                    last = pe.matmul(bank[6 + c][:, b * P:(b + 1) * P], msg[:, c * CB + b, :],
                                     aff_t[:, c * CB + b, :], start=True, stop=True)
                last.then_inc(nmp_ps, 1)

            def head(g):
                for c in range(NCH):
                    cs = slice(c * CW, (c + 1) * CW)
                    pe.wait_ge(h_lo_ready, NCH * g + c + 1)
                    three(bank[c][:], CONV1, h_hi[:, cs], h_lo[:, cs], True, True).then_inc(conv1_ps, 1)
                for c in range(NCH):
                    cs = slice(c * CW, (c + 1) * CW)
                    previous(pe, r_ready, NCH * g) if c == 0 else previous(pe, v_ready, NCH * g)
                    dst = bank[4 + c][0:96, :]
                    pe.matmul(dst, wt_hi[:, SE, 0:96], h_hi[:, cs], start=True, stop=False)
                    pe.matmul(dst, wt_hi[:, SE, 0:96], h_lo[:, cs], start=False, stop=False)
                    pe.matmul(dst, wt_lo[:, SE, 0:96], h_hi[:, cs], start=False, stop=True).then_inc(s_ps, 1)
                for c in range(NCH):
                    previous(pe, z_ready, NCH * (g - 1) + c + 1)
                    pe.matmul(bank[Z_BANK[c]][:], ones[:], bm[:], start=True, stop=False)
                    for b in range(CB):
                        hs = slice((c * CB + b) * P, (c * CB + b + 1) * P)
                        last = pe.matmul(bank[Z_BANK[c]][:, b * P:(b + 1) * P], hf[:, hs], wt_msg[:],
                                         start=False, stop=(b == CB - 1))
                    last.then_inc(msg_ps, 1)

            def distance(g, c):
                pe.wait_ge(s_ready, 2 * (NCH * g + c + 1))
                pe.wait_ge(sq_ready, 2 * (NCH * g + c + 1))
                for b in range(CB):
                    last = pe.matmul(bank[4 + c][:, b * P:(b + 1) * P], left[:, c * CB + b, :],
                                     right[:, c * CB + b, :], start=True, stop=True)
                last.then_inc(dist_ps, 1)

            def body(g, ahead):
                for q in range(9):
                    sub_conv(g, q)
                    if q == 1:
                        distance(g, 0)
                        distance(g, 1)
                    if q in (4, 5):
                        a_transpose(g, q - 4)
                    if q in (6, 7):
                        gather(g, q - 6)
                gates(g, 0, ahead)
                gates(g, 1, ahead)
                out_transpose(g, 0)
                if ahead:
                    head(g + 1)
                out_transpose(g, 1)

            head(0)
            body(0, True)
            with pe.Fori(1, NG - 1) as g:
                body(g, True)
            body(NG - 1, False)


def previous(engine, semaphore, count):
    if not isinstance(count, int) or count > 0:
        engine.wait_ge(semaphore, count)


_INS = ["x", "adj", "w_se", "b_se", "conv1_w", "bn1_g", "bn1_b", "bn1_m", "bn1_v", "conv2_w", "bn2_g", "bn2_b",
        "bn2_m", "bn2_v", "w_msg", "b_msg", "w_ih", "b_ih", "w_hh", "b_hh"]


def kernel(**inputs):
    import numpy as np
    import concourse.bacc as bacc
    from concourse.bass_utils import run_bass_kernel_spmd

    nc = bacc.Bacc("TRN2", target_bir_lowering=False, num_devices=1)
    arrays, args = {}, []
    for name in _INS:
        a = np.ascontiguousarray(inputs[name if name in ("x", "adj") else "L0_gnn_" + name])
        arrays[f"in_{name}"] = a
        args.append(nc.dram_tensor(f"in_{name}", a.shape, mybir.dt.from_np(a.dtype), kind="ExternalInput").ap())
    out = nc.dram_tensor("out", (NB, P, P), F32, kind="ExternalOutput").ap()
    gnn_kernel(nc, *args, out)
    return run_bass_kernel_spmd(nc, [arrays], core_ids=[0]).results[0]["out"]
```

```python
from contextlib import ExitStack

import concourse.bass as bass
from concourse import mybir

F32 = mybir.dt.float32
F32R = mybir.dt.float32r
ALU = mybir.AluOpType
ACT = mybir.ActivationFunctionType

P = 128
NB = 64
GB = 8
CB = 4
NCH = GB // CB
NG = NB // GB
CW = CB * P
GW = GB * P
TAPS = 17
EPS = 1e-5

CPAD, UPAD, VPAD = P + 8, P // 2 + 4, P // 4 + 4
HALF, QUART = P // 2, P // 4
ORDER = "bac"
LEN1 = {"a": (TAPS + 1) // 2, "b": (TAPS + 1) // 2, "c": TAPS // 2}


def sub_taps():
    at, out = 0, []
    for u in ORDER:
        for v in ORDER:
            n = LEN1[u] // 2 if v == "c" else (LEN1[u] + 1) // 2
            out.append((at, n))
            at += n
    return out, at


SUBS, NT = sub_taps()
CONV1, MSG = NT, NT + 1
def IH(gate, part):
    return NT + 2 + 2 * gate + part
def HH(gate):
    return NT + 8 + gate
SE = NT + 11
NBLK = NT + 12
R, Z, N = 0, 1, 2
Z_BANK = (6, 2)
S_ROWS = (0, 32, 64)
SK = 67
(G1, G2, B1, B2, M1, M2, V1, V2, BIR, BIZ, BIN, BHR, BHZ, BHN,
 SC1, SC2, C1B, C2B, HR, HZ, HN, T1) = range(22)


def gnn_kernel(nc, x, adj, w_se, b_se, conv1_w, bn1_g, bn1_b, bn1_m, bn1_v, conv2_w, bn2_g, bn2_b,
               bn2_m, bn2_v, w_msg, b_msg, w_ih, b_ih, w_hh, b_hh, out):
    ctx = ExitStack()
    with ctx:
        def sb(name, shape, dt=F32):
            return ctx.enter_context(nc.sbuf_tensor(name, shape, dt))

        def sem(name):
            return ctx.enter_context(nc.semaphore(name))

        ident = sb("ident", [P, P])
        par = sb("par", [P, 24])
        se_b = sb("se_b", [SK, 1])
        wt_hi = sb("wt_hi", [P, NBLK, P], F32R)
        wt_lo = sb("wt_lo", [P, NBLK, P], F32R)
        bm = sb("bm", [P, P])
        xin = sb("xin", [P, NCH, CB, P])
        xres = sb("xres", [P, NCH, CB, P])
        outb = sb("outb", [P, NCH, CB, P])
        stats = sb("stats", [P, GB, 6])
        mv = sb("mv", [P, GB, 2])
        vpe = sb("vpe", [P, GB])
        rstd = sb("rstd", [P, GB])
        neg_half = sb("neg_half", [P, GB])
        hn = sb("hn", [P, NCH, CB, P])
        hf = sb("hf", [P, GW])
        hf2 = sb("hf2", [P, GW])
        h_hi = sb("h_hi", [P, GW], F32R)
        h_lo = sb("h_lo", [P, GW], F32R)
        cp = sb("cp", [P, GB, CPAD])
        ua = sb("ua", [P, GB, UPAD])
        uc = sb("uc", [P, GB, UPAD])
        vt = sb("vt", [P, 6, GB, QUART + 1])
        v_hi = sb("v_hi", [P, 9, GB, VPAD], F32R)
        v_lo = sb("v_lo", [P, 9, GB, VPAD], F32R)
        mbs = sb("mbs", [P, GB, QUART])
        ma = sb("ma", [P, GB, HALF])
        mb = sb("mb", [P, GB, HALF])
        mc = sb("mc", [P, GB, HALF])
        xc_hi = sb("xc_hi", [P, GW], F32R)
        xc_lo = sb("xc_lo", [P, GW], F32R)
        left = sb("left", [SK, GB, P])
        right = sb("right", [SK, GB, P])
        msg = sb("msg", [P, GB, P])
        aff_t = sb("aff_t", [P, GB, P])
        wt_msg = sb("wt_msg", [P, P])
        n_hi = sb("n_hi", [P, GW], F32R)
        n_lo = sb("n_lo", [P, GW], F32R)
        scratch = sb("scratch", [P, 9216])
        spans = [0, 0]

        def cut(width, which):
            a = spans[which]
            spans[which] += width
            assert spans[which] <= 9216
            return scratch[:, a:a + width]

        w2 = cut(P * TAPS, 0).rearrange("p (c k) -> p c k", k=TAPS)
        f1 = {u: cut(LEN1[u] * P, 0).rearrange("p (k c) -> p k c", c=P) for u in ORDER}
        fs = {u: cut(LEN1[u] // 2 * P, 0).rearrange("p (k c) -> p k c", c=P) for u in ORDER}
        w1_raw, msg_raw, se_raw = cut(P, 0), cut(P, 0), cut(P, 0)
        ih_raw = cut(6 * P, 0).rearrange("p (g k c) -> p g k c", g=3, k=2)
        hh_raw = cut(3 * P, 0).rearrange("p (g c) -> p g c", g=3)
        mask = cut(GW, 1).rearrange("p (b m) -> p b m", m=P)
        aff = cut(GW, 1).rearrange("p (b m) -> p b m", m=P)
        y = cut(GW, 1)
        pa = cut(GB * HALF, 1).rearrange("p (b j) -> p b j", j=HALF)
        pc = cut(GB * HALF, 1).rearrange("p (b j) -> p b j", j=HALF)
        gn = [cut(CW, 1) for _ in range(NCH)]
        gr = [cut(CW, 1) for _ in range(NCH)]
        gz = [cut(CW, 1) for _ in range(NCH)]
        gw = [cut(CW, 1) for _ in range(NCH)]

        bank = [ctx.enter_context(nc.psum_tensor(f"bank{i}", [P, CW], F32)) for i in range(8)]

        w1_landed, ih_landed, w_landed, se_landed, seb_landed, c2_landed = (
            sem("w1_landed"), sem("ih_landed"), sem("w_landed"), sem("se_landed"), sem("seb_landed"),
            sem("c2_landed"))
        bn_landed, bn_off_landed, gb_landed, bm_landed = sem("bn_landed"), sem("bn_off_landed"), sem("gb_landed"), sem("bm_landed")
        x_landed = [sem(f"x_landed{c}") for c in range(NCH)]
        xres_landed = [sem(f"xres_landed{c}") for c in range(NCH)]
        mask_landed = sem("mask_landed")
        out_stored = [sem(f"out_stored{c}") for c in range(NCH)]
        pool_set, pool_par, ident_ready = sem("pool_set"), sem("pool_par"), sem("ident_ready")
        pads_set, bias_set, w1_scaled, f1_ac, f1_b, fs_b, fs_ac = (
            sem("pads_set"), sem("bias_set"), sem("w1_scaled"), sem("f1_ac"), sem("f1_b"), sem("fs_b"),
            sem("fs_ac"))
        wt_ps, wt_hi_ready, wt_lo_ready = sem("wt_ps"), sem("wt_hi_ready"), sem("wt_lo_ready")
        stats_ready, mv_ready, rstd_ready, vpe_ready, hn_ready = (
            sem("stats_ready"), sem("mv_ready"), sem("rstd_ready"), sem("vpe_ready"), sem("hn_ready"))
        ht_ps, h_used, hf_ready, h_hi_ready, h_lo_ready, hf2_ready = (
            sem("ht_ps"), sem("h_used"), sem("hf_ready"), sem("h_hi_ready"), sem("h_lo_ready"), sem("hf2_ready"))
        conv1_ps, c_ready, u_ready, t_ready, v_hi_ready, v_lob_ready, v_loac_ready = (
            sem("conv1_ps"), sem("c_ready"), sem("u_ready"), sem("t_ready"), sem("v_hi_ready"),
            sem("v_lob_ready"), sem("v_loac_ready"))
        conv2_ps, mbs_ready, m_ready, p_ready, y_ready, xc_hi_ready, xc_lo_ready = (
            sem("conv2_ps"), sem("mbs_ready"), sem("m_ready"), sem("p_ready"), sem("y_ready"),
            sem("xc_hi_ready"), sem("xc_lo_ready"))
        s_ps, s_ready, sq_ready, right_ready, dist_ps, e_ready, a_ready = (
            sem("s_ps"), sem("s_ready"), sem("sq_ready"), sem("right_ready"), sem("dist_ps"),
            sem("e_ready"), sem("a_ready"))
        at_ps, at_ready, msg_ps, msg_sum_ready, msg_ready = (
            sem("at_ps"), sem("at_ready"), sem("msg_ps"), sem("msg_sum_ready"), sem("msg_ready"))
        nmp_ps, n_hi_ready, n_lo_ready = sem("nmp_ps"), sem("n_hi_ready"), sem("n_lo_ready")
        ghn_ps, r_ps, gin_ps, z_ps, ghn_ready, r_ready, z_ready = (
            sem("ghn_ps"), sem("r_ps"), sem("gin_ps"), sem("z_ps"), sem("ghn_ready"), sem("r_ready"),
            sem("z_ready"))
        rg_ready, v_ready, cand_ready, diff_ready, zd_ready, o_ready, ot_ps, out_ready = (
            sem("rg_ready"), sem("v_ready"), sem("cand_ready"), sem("diff_ready"), sem("zd_ready"),
            sem("o_ready"), sem("ot_ps"), sem("out_ready"))

        x_v = x.rearrange("(k b) n d -> k n b d", b=CB)
        out_v = out.rearrange("(k b) n d -> k n b d", b=CB)
        adj_v = adj.rearrange("(g b) n m -> g n b m", b=GB)

        def tap1(u, k):
            return f1["a" if u == "b" and k >= LEN1["c"] else u][:, k, :]

        def tap2(u, v, k):
            if v == "b" and 2 * k + 1 < LEN1[u]:
                return fs[u][:, k, :]
            return tap1(u, 2 * k + (v == "c"))

        blocks = [tap2(u, v, k) for q, (u, v) in enumerate((u, v) for u in ORDER for v in ORDER)
                  for k in range(SUBS[q][1])]
        blocks += [w1_raw, msg_raw] + [ih_raw[:, g, k, :] for g in range(3) for k in range(2)]
        blocks += [hh_raw[:, g, :] for g in range(3)] + [se_raw]
        assert len(blocks) == NBLK
        lots = [list(range(i, min(i + CB, NBLK))) for i in range(NT, NBLK, CB)]
        plain = len(lots)
        assert plain == 3 and lots[0][0] == CONV1
        lots[0], lots[1] = lots[1], lots[0]
        lots += [list(range(i, min(i + CB, NT))) for i in range(0, NT, CB)]
        assert len(lots) == plain + 10
        LOT_BANK = (2, 3, 4) + (0, 1, 7, 3, 7) + (3, 7, 6, 3, 7)
        EARLY = plain + 4

        def lot_of(blk):
            return plain + blk // CB


        def vec(a):
            return a.rearrange("(p a) -> p a", a=1)

        def v_src(q):
            u, v = ORDER[q // 3], ORDER[q % 3]
            if v != "b":
                return vt[:, 2 * (q // 3) + (v == "c"), :, :]
            return u_view(u, -1, 1 + QUART, 1)

        def u_view(u, first, count, phase):
            if u == "b":
                a = 2 * (2 * first + phase) + 1 + 4
                return cp[:, :, a:a + 4 * (count - 1) + 1:4]
            a = 2 * first + phase + 2
            return (ua if u == "a" else uc)[:, :, a:a + 2 * (count - 1) + 1:2]

        block = ctx.enter_context(nc.Block())

        @block.sync
        def _(sp):
            def load_x(g, c):
                sp.dma_start(xin[:, c], x_v[NCH * g + c]).then_inc(x_landed[c], 16)

            def load_mask(g):
                sp.dma_start(mask, adj_v[g]).then_inc(mask_landed, 16)

            for c in range(NCH):
                load_x(0, c)
            sp.dma_start(w1_raw, conv1_w.rearrange("o c k -> o (c k)")).then_inc(w1_landed, 16)
            sp.dma_start(ih_raw, w_ih.rearrange("(g p) (k c) -> p g k c", g=3, k=2)).then_inc(ih_landed, 16)
            sp.dma_start(w2, conv2_w).then_inc(c2_landed, 16)
            sp.dma_start(msg_raw, w_msg).then_inc(w_landed, 16)
            sp.dma_start(hh_raw, w_hh.rearrange("(g p) c -> p g c", g=3)).then_inc(w_landed, 16)
            for i, p in ((M1, bn1_m), (M2, bn2_m), (B1, bn1_b), (B2, bn2_b)):
                sp.dma_start(par[:, i:i + 1], vec(p)).then_inc(bn_off_landed, 16)
            sp.wait_ge(pool_set, 2)
            for r in S_ROWS:
                sp.dma_start(se_b[r:r + 3, :], vec(b_se)).then_inc(seb_landed, 16)
            sp.dma_start(bm[:], b_msg.partition_broadcast(P)).then_inc(bm_landed, 16)
            for i in range(3):
                sp.dma_start(par[:, BIR + i:BIR + i + 1], vec(b_ih[i * P:(i + 1) * P])).then_inc(gb_landed, 16)
                sp.dma_start(par[:, BHR + i:BHR + i + 1], vec(b_hh[i * P:(i + 1) * P])).then_inc(gb_landed, 16)
            sp.wait_ge(hn_ready, NCH)
            for c in range(NCH):
                load_x(1, c)
            sp.wait_ge(f1_ac, 2)
            load_mask(0)

            def body(g, ahead, ahead2):
                for c in range(NCH):
                    previous(sp, out_ready, NCH * g)
                    sp.dma_start(xres[:, c], x_v[NCH * g + c]).then_inc(xres_landed[c], 16)
                if ahead:
                    sp.wait_ge(a_ready, NCH * g + NCH)
                    load_mask(g + 1)
                if ahead2:
                    sp.wait_ge(hn_ready, NCH * g + 2 * NCH)
                    for c in range(NCH):
                        load_x(g + 2, c)
                for c in range(NCH):
                    sp.wait_ge(out_ready, NCH * g + c + 1)
                    sp.dma_start(out_v[NCH * g + c], outb[:, c]).then_inc(out_stored[c], 16)

            body(0, True, True)
            with sp.Fori(1, NG - 2) as g:
                body(g, True, True)
            body(NG - 2, True, False)
            body(NG - 1, False, False)
            for c in range(NCH):
                sp.wait_ge(out_stored[c], 16 * NG)

        @block.gpsimd
        def _(pool):
            pool.memset(se_raw, 0.0).then_inc(pool_set, 1)
            pool.memset(se_b[:], 0.0).then_inc(pool_set, 1)
            pool.memset(ident[:], 0.0).then_inc(pool_set, 1)
            pool.memset(neg_half[:], -0.5).then_inc(pool_set, 1)
            pool.memset(right[:], 0.0).then_inc(pool_set, 1)
            pool.wait_ge(pool_set, 5)
            pool.affine_select(out=ident[:], in_=ident[:], compare_op=ALU.not_equal, fill=1.0, base=0,
                               pattern=[[-1, P]], channel_multiplier=1).then_inc(ident_ready, 1)
            for r in S_ROWS:
                pool.dma_start(se_raw[r:r + 3, :], w_se).then_inc(se_landed, 16)

            def ln_scale(n):
                pool.wait_ge(vpe_ready, n)
                pool.tensor_tensor(rstd[:], vpe[:], neg_half[:], ALU.pow).then_inc(rstd_ready, 1)

            def cols(i):
                return par[:, i:i + 2]

            pool.wait_ge(ident_ready, 1)
            ln_scale(1)
            pool.wait_ge(bn_landed, 4 * 16)
            pool.tensor_scalar(cols(V1), cols(V1), EPS, None, ALU.add).then_inc(pool_par, 1)
            pool.wait_ge(pool_par, 1)
            pool.tensor_tensor(cols(SC1), cols(V1), neg_half[:, 0:2], ALU.pow).then_inc(pool_par, 1)
            pool.wait_ge(pool_par, 2)
            pool.tensor_tensor(cols(SC1), cols(SC1), cols(G1), ALU.mult).then_inc(pool_par, 1)
            pool.wait_ge(pool_par, 3)
            pool.wait_ge(bn_off_landed, 4 * 16)
            pool.tensor_tensor(cols(C1B), cols(M1), cols(SC1), ALU.mult).then_inc(pool_par, 1)
            pool.wait_ge(pool_par, 4)
            pool.tensor_tensor(cols(C1B), cols(B1), cols(C1B), ALU.subtract).then_inc(pool_par, 1)
            pool.wait_ge(f1_ac, 2)
            for u in "ac":
                h = LEN1[u] // 2
                pool.tensor_tensor(fs[u], f1[u][:, 0:2 * h:2, :], f1[u][:, 1:2 * h:2, :],
                                   ALU.add).then_inc(fs_ac, 1)

            def level1(g):
                pool.wait_ge(c_ready, NCH * g + NCH)
                previous(pool, t_ready, 6 * g)
                previous(pool, v_hi_ready, 9 * g)
                n = UPAD - 1
                pool.tensor_tensor(ua[:, :, 0:n], cp[:, :, 0:2 * n:2], cp[:, :, 1:2 * n:2],
                                   ALU.subtract).then_inc(u_ready, 1)
                pool.tensor_tensor(uc[:, :, 0:n], cp[:, :, 2:2 * n + 2:2], cp[:, :, 1:2 * n:2],
                                   ALU.subtract).then_inc(u_ready, 1)

            def v_low(g, q):
                pool.wait_ge(v_hi_ready, 9 * g + q + 1)
                pool.tensor_tensor(v_lo[:, q, :, 1:QUART + 2], v_src(q), v_hi[:, q, :, 1:QUART + 2],
                                   ALU.subtract).then_inc(v_loac_ready, 1)

            def body(g, ahead, first=False):
                level1(g)
                for q in range(3, 6):
                    v_low(g, q)
                for c in range(NCH):
                    cs = slice(c * CB, (c + 1) * CB)
                    pool.wait_ge(e_ready, NCH * g + c + 1)
                    if c == 0:
                        pool.wait_ge(mask_landed, 16 * g + 16)
                    pool.tensor_tensor(aff[:, cs, :], aff[:, cs, :], mask[:, cs, :],
                                       ALU.mult).then_inc(a_ready, 1)
                for q in range(6, 9):
                    v_low(g, q)
                if ahead:
                    ln_scale(g + 2)
                if first:
                    pool.wait_ge(wt_ps, len(lots))
                pool.wait_ge(m_ready, 6 * g + 2)
                hv = hf[:].rearrange("p (b j t) -> p b j t", j=HALF, t=2)
                previous(pool, y_ready, 2 * g)
                pool.tensor_tensor(pa, hv[:, :, :, 0], mb[:], ALU.add).then_inc(p_ready, 1)
                pool.tensor_tensor(pc, hv[:, :, :, 1], mb[:], ALU.add).then_inc(p_ready, 1)
                for c in range(NCH):
                    pool.wait_ge(cand_ready, NCH * g + c + 1)
                    previous(pool, ot_ps, NCH * g)
                    pool.tensor_tensor(gw[c], hf2[:, c * CW:(c + 1) * CW], gn[c],
                                       ALU.subtract).then_inc(diff_ready, 1)

            body(0, True, first=True)
            with pool.Fori(1, NG - 1) as g:
                body(g, True)
            body(NG - 1, False)

        @block.scalar
        def _(act):
            for i, p in ((V1, bn1_v), (V2, bn2_v), (G1, bn1_g), (G2, bn2_g)):
                act.dma_start(par[:, i:i + 1], vec(p)).then_inc(bn_landed, 16)

            def h_rows(g, c, first=False):
                cs = slice(c * CW, (c + 1) * CW)
                act.wait_ge(ht_ps, NCH * g + c + 1)
                if not first:
                    previous(act, hf2_ready, g)
                    previous(act, p_ready, 2 * g)
                    act.wait_ge(msg_ps, NCH * g)
                    act.wait_ge(h_used, NCH * (g - 1) + c + 1)
                act.activation(hf[:, cs], bank[c][:], ACT.Relu).then_inc(hf_ready, 1)
                act.activation(h_hi[:, cs], bank[c][:], ACT.Relu).then_inc(h_hi_ready, 1)

            def lot_high(n):
                lot = lots[n]
                act.wait_ge(wt_ps, n + 1)
                w, src = len(lot), bank[LOT_BANK[n]]
                if MSG in lot:
                    a = (MSG - lot[0]) * P
                    act.activation(wt_msg[:], src[:, a:a + P], ACT.Copy)
                act.activation(wt_hi[:, lot[0]:lot[0] + w, :], src[:, 0:w * P], ACT.Copy).then_inc(wt_hi_ready, 1)

            def v_high(g, q):
                u, v = ORDER[q // 3], ORDER[q % 3]
                if v != "b":
                    act.wait_ge(t_ready, 6 * g + 2 * (q // 3) + (v == "c") + 1)
                elif u != "b":
                    act.wait_ge(u_ready, 2 * g + "ac".index(u) + 1)
                else:
                    act.wait_ge(c_ready, NCH * g + NCH)
                previous(act, conv2_ps, 9 * g)
                act.activation(v_hi[:, q, :, 1:QUART + 2], v_src(q), ACT.Copy).then_inc(v_hi_ready, 1)

            def m_shared(g, u):
                act.wait_ge(conv2_ps, 9 * g + 3 * u + 1)
                previous(act, m_ready, 6 * g + 2 * u)
                src = bank[0][:, 0:GB * QUART].rearrange("p (b l) -> p b l", l=QUART)
                if u == 0:
                    act.activation(mbs[:], src, ACT.Identity, bias=par[:, C2B:C2B + 1]).then_inc(mbs_ready, 1)
                else:
                    act.activation(mbs[:], src, ACT.Copy).then_inc(mbs_ready, 1)

            def at_rows(g, c):
                act.wait_ge(at_ps, NCH * g + c + 1)
                act.activation(aff_t[:, c * CB:(c + 1) * CB, :], bank[3][:], ACT.Copy).then_inc(at_ready, 1)

            def n_high(g, c):
                act.wait_ge(nmp_ps, NCH * g + c + 1)
                act.activation(n_hi[:, c * CW:(c + 1) * CW], bank[6 + c][:], ACT.Copy).then_inc(n_hi_ready, 1)

            def squares(g, c):
                act.wait_ge(s_ps, NCH * g + c + 1)
                for dst, r in ((right, 32), (left, 64)):
                    act.activation(dst[r:r + 3, c * CB:(c + 1) * CB, :], bank[4 + c][r:r + 3, :], ACT.Square,
                                   bias=se_b[r:r + 3, 0:1]).then_inc(sq_ready, 1)

            def right_rows(g, c):
                act.wait_ge(s_ready, NCH * g + c + 1)
                act.activation(right[0:3, c * CB:(c + 1) * CB, :], bank[4 + c][0:3, :], ACT.Identity,
                               bias=se_b[0:3, 0:1]).then_inc(right_ready, 1)

            def conv1_rows(g):
                for c in range(NCH):
                    act.wait_ge(conv1_ps, NCH * g + c + 1)
                    previous(act, u_ready, 2 * g)
                    previous(act, v_lob_ready, 3 * g)
                    act.activation(cp[:, c * CB:(c + 1) * CB, 4:4 + P],
                                   bank[c][:].rearrange("p (b n) -> p b n", n=P), ACT.Relu,
                                   bias=par[:, C1B:C1B + 1]).then_inc(c_ready, 1)

            def head(g, first=False):
                for q in range(3):
                    v_high(g, q)
                if first:
                    lot_high(plain)
                    lot_high(plain + 1)
                squares(g, 0)
                squares(g, 1)
                right_rows(g, 0)
                right_rows(g, 1)

            def body(g, ahead, first=False):
                v_high(g, 3)
                if first:
                    for n in range(EARLY, EARLY + 3):
                        lot_high(n)
                for c in range(NCH):
                    act.wait_ge(msg_sum_ready, NCH * g + c + 1)
                    m = msg[:, c * CB:(c + 1) * CB, :]
                    act.activation(m, m, ACT.Relu).then_inc(msg_ready, 1)
                m_shared(g, 0)
                v_high(g, 4)
                v_high(g, 5)
                previous(act, diff_ready, NCH * g)
                act.activation(hf2[:], hf[:], ACT.Copy).then_inc(hf2_ready, 1)
                for c in range(NCH):
                    act.wait_ge(dist_ps, NCH * g + c + 1)
                    act.activation(aff[:, c * CB:(c + 1) * CB, :], bank[4 + c][:], ACT.Exp,
                                   scale=2.0).then_inc(e_ready, 1)
                for q in range(6, 9):
                    v_high(g, q)
                if first:
                    for n in range(EARLY + 3, len(lots)):
                        lot_high(n)
                m_shared(g, 1)
                at_rows(g, 0)
                at_rows(g, 1)
                m_shared(g, 2)
                n_high(g, 0)
                n_high(g, 1)
                for c in range(NCH):
                    act.wait_ge(y_ready, 2 * g + 2)
                    cs = slice(c * CW, (c + 1) * CW)
                    act.activation(xc_hi[:, cs], y[:, cs], ACT.Relu).then_inc(xc_hi_ready, 1)
                for c in range(NCH):
                    previous(act, o_ready, NCH * g)
                    act.wait_ge(ghn_ps, NCH * g + c + 1)
                    act.activation(gn[c], bank[3][:], ACT.Identity, bias=par[:, HN:HN + 1],
                                   scale=0.5).then_inc(ghn_ready, 1)
                    if ahead:
                        h_rows(g + 1, c)
                    act.wait_ge(r_ps, NCH * g + c + 1)
                    act.activation(gr[c], bank[4][:], ACT.Tanh, bias=par[:, HR:HR + 1],
                                   scale=0.5).then_inc(r_ready, 1)
                    act.wait_ge(v_ready, NCH * g + c + 1)
                    act.activation(gn[c], gn[c], ACT.Tanh, bias=par[:, BIN:BIN + 1]).then_inc(cand_ready, 1)
                    if ahead and c == NCH - 1:
                        conv1_rows(g + 1)
                    act.wait_ge(z_ps, NCH * g + c + 1)
                    act.activation(gz[c], bank[Z_BANK[c]][:], ACT.Tanh, bias=par[:, HZ:HZ + 1],
                                   scale=0.5).then_inc(z_ready, 1)
                if ahead:
                    head(g + 1)

            lot_high(0)
            act.wait_ge(pool_par, 3)
            act.wait_ge(c2_landed, 16)
            w2k = w2.rearrange("p c k -> p k c")

            def taps(i):
                act.activation(f1["ac"[i]], w2k[:, i:TAPS:2, :], ACT.Copy,
                               scale=par[:, SC2:SC2 + 1]).then_inc(f1_ac, 1)

            taps(0)
            h_rows(0, 0, first=True)
            lot_high(1)
            h_rows(0, 1, first=True)
            lot_high(2)
            taps(1)
            act.wait_ge(pads_set, 9)
            act.wait_ge(pool_par, 5)
            act.wait_ge(seb_landed, 3 * 16)
            conv1_rows(0)
            head(0, first=True)
            for n in range(plain + 2, EARLY):
                lot_high(n)
            act.wait_ge(bias_set, 3)
            body(0, True, first=True)
            with act.Fori(1, NG - 1) as g:
                body(g, True)
            body(NG - 1, False)

        @block.vector
        def _(dve):
            def ln_stats(g):
                for c in range(NCH):
                    dve.wait_ge(x_landed[c], 16 * g + 16)
                    for b in range(CB):
                        last = dve.bn_stats(stats[:, c * CB + b, :], xin[:, c, b, :])
                last.then_inc(stats_ready, 1)

            def ln_moments(g):
                for b in range(GB):
                    last = dve.bn_aggr(mv[:, b, :], stats[:, b, :])
                last.then_inc(mv_ready, 1)
                dve.wait_ge(mv_ready, g + 1)
                previous(dve, rstd_ready, g)
                dve.tensor_scalar(vpe[:], mv[:, :, 1], EPS, None, ALU.add).then_inc(vpe_ready, 1)

            def ln_rows(g):
                dve.wait_ge(rstd_ready, g + 1)
                previous(dve, ht_ps, NCH * g)
                for b in range(GB):
                    c, i = b // CB, b % CB
                    last = dve.tensor_scalar(hn[:, c, i, :], xin[:, c, i, :], mv[:, b, 0:1], rstd[:, b:b + 1],
                                             ALU.subtract, ALU.mult)
                    if i == CB - 1:
                        last.then_inc(hn_ready, 1)

            def h_low(g, c):
                cs = slice(c * CW, (c + 1) * CW)
                dve.wait_ge(h_hi_ready, NCH * g + c + 1)
                dve.tensor_tensor(h_lo[:, cs], hf[:, cs], h_hi[:, cs], ALU.subtract).then_inc(h_lo_ready, 1)

            dve.memset(cp[:, :, 0:4], 0.0).then_inc(pads_set, 1)
            dve.memset(cp[:, :, 4 + P:CPAD], 0.0).then_inc(pads_set, 1)
            for v in (v_hi, v_lo):
                dve.memset(v[:, :, :, 0:1].bitcast(F32), 0.0).then_inc(pads_set, 1)
                dve.memset(v[:, :, :, QUART + 2:VPAD].bitcast(F32), 0.0).then_inc(pads_set, 1)
            dve.memset(left[:], 0.0).then_inc(pads_set, 1)
            ln_stats(0)
            dve.wait_ge(stats_ready, 1)
            ln_moments(0)
            dve.wait_ge(pads_set, 7)
            dve.memset(left[32:35], -0.5).then_inc(pads_set, 1)
            ln_rows(0)
            dve.wait_ge(pool_par, 3)
            dve.wait_ge(w1_landed, 16)
            dve.tensor_scalar(w1_raw, w1_raw, par[:, SC1:SC1 + 1], None, ALU.mult).then_inc(w1_scaled, 1)
            def lot_low(n):
                lot = lots[n]
                dve.wait_ge(wt_hi_ready, n + 1)
                w = len(lot)
                bs = slice(lot[0], lot[0] + w)
                dve.tensor_tensor(wt_lo[:, bs, :], bank[LOT_BANK[n]][:, 0:w * P].rearrange("p (b c) -> p b c", c=P),
                                  wt_hi[:, bs, :], ALU.subtract).then_inc(wt_lo_ready, 1)

            def level2(g, u):
                name = ORDER[u]
                if name == "b":
                    dve.wait_ge(c_ready, NCH * g + NCH)
                else:
                    dve.wait_ge(u_ready, 2 * g + "ac".index(name) + 1)
                previous(dve, v_hi_ready, 9 * g)
                previous(dve, v_loac_ready, 6 * g)
                n = QUART + 1
                odd = u_view(name, -1, n, 1)
                dve.tensor_tensor(vt[:, 2 * u], u_view(name, -1, n, 0), odd, ALU.subtract).then_inc(t_ready, 1)
                dve.tensor_tensor(vt[:, 2 * u + 1], u_view(name, 0, n, 0), odd, ALU.subtract).then_inc(t_ready, 1)

            def join(g, u):
                dst = (mb, ma, mc)[u]
                dst = dst[:].rearrange("p b (l t) -> p b l t", t=2)
                dve.wait_ge(mbs_ready, 3 * g + u + 1)
                for t in range(2):
                    dve.wait_ge(conv2_ps, 9 * g + 3 * u + 2 + t)
                    if u == 0 and t == 0:
                        previous(dve, p_ready, 2 * g)
                    src = bank[1 + t][:, 0:GB * QUART].rearrange("p (b l) -> p b l", l=QUART)
                    dve.tensor_tensor(dst[:, :, :, t], src, mbs[:], ALU.add).then_inc(m_ready, 1)

            def join_y(g, t):
                dve.wait_ge(m_ready, 6 * g + 4 + 2 * t)
                dve.wait_ge(p_ready, 2 * g + t + 1)
                yv = y.rearrange("p (b j t) -> p b j t", j=HALF, t=2)
                dve.tensor_tensor(yv[:, :, :, t], (ma, mc)[t][:], (pa, pc)[t], ALU.add).then_inc(y_ready, 1)

            def left_rows(g, c):
                dve.wait_ge(s_ps, NCH * g + c + 1)
                dve.tensor_scalar(left[0:3, c * CB:(c + 1) * CB, :],
                                  bank[4 + c][0:3, :].rearrange("p (b n) -> p b n", n=P),
                                  se_b[0:3, 0:1], None, ALU.add).then_inc(s_ready, 1)

            def v_low(g, q):
                dve.wait_ge(v_hi_ready, 9 * g + q + 1)
                dve.tensor_tensor(v_lo[:, q, :, 1:QUART + 2], v_src(q), v_hi[:, q, :, 1:QUART + 2],
                                  ALU.subtract).then_inc(v_lob_ready, 1)

            def body(g, ahead, first=False):
                def n_low(c):
                    cs = slice(c * CW, (c + 1) * CW)
                    dve.wait_ge(n_hi_ready, NCH * g + c + 1)
                    dve.tensor_tensor(n_lo[:, cs], bank[6 + c][:], n_hi[:, cs], ALU.subtract).then_inc(n_lo_ready, 1)

                level2(g, 1)
                for c in range(NCH):
                    dve.wait_ge(msg_ps, NCH * g + c + 1)
                    dve.tensor_tensor(msg[:, c * CB:(c + 1) * CB, :],
                                      bank[Z_BANK[c]][:].rearrange("p (b d) -> p b d", d=P),
                                      bm[:].unsqueeze(1).broadcast_to([P, CB, P]), ALU.add).then_inc(msg_sum_ready, 1)
                if first:
                    for n in range(EARLY, EARLY + 3):
                        lot_low(n)
                level2(g, 2)
                if ahead:
                    ln_stats(g + 1)
                    dve.wait_ge(stats_ready, g + 2)
                join(g, 0)
                if first:
                    for n in range(EARLY + 3, len(lots)):
                        lot_low(n)
                if ahead:
                    ln_moments(g + 1)
                join(g, 1)
                if ahead:
                    ln_rows(g + 1)
                join_y(g, 0)
                n_low(0)
                join(g, 2)
                join_y(g, 1)
                n_low(1)
                for c in range(NCH):
                    cs = slice(c * CW, (c + 1) * CW)
                    dve.wait_ge(xc_hi_ready, NCH * g + c + 1)
                    dve.scalar_tensor_tensor(out=xc_lo[:, cs], in0=y[:, cs], scalar=0.0, in1=xc_hi[:, cs],
                                             op0=ALU.max, op1=ALU.subtract).then_inc(xc_lo_ready, 1)
                def reset(c):
                    dve.wait_ge(r_ready, NCH * g + c + 1)
                    dve.scalar_tensor_tensor(out=gn[c], in0=gr[c], scalar=1.0, in1=gn[c], op0=ALU.add,
                                             op1=ALU.mult).then_inc(rg_ready, 1)
                    dve.wait_ge(rg_ready, NCH * g + c + 1)
                    dve.wait_ge(gin_ps, NCH * g + c + 1)
                    dve.tensor_tensor(gn[c], bank[5][:], gn[c], ALU.add).then_inc(v_ready, 1)

                def gated(c):
                    dve.wait_ge(z_ready, NCH * g + c + 1)
                    dve.wait_ge(diff_ready, NCH * g + c + 1)
                    dve.scalar_tensor_tensor(out=gw[c], in0=gz[c], scalar=1.0, in1=gw[c], op0=ALU.add,
                                             op1=ALU.mult).then_inc(zd_ready, 1)

                def update(c):
                    dve.wait_ge(zd_ready, NCH * g + c + 1)
                    dve.scalar_tensor_tensor(out=gw[c], in0=gw[c], scalar=0.5, in1=gn[c], op0=ALU.mult,
                                             op1=ALU.add).then_inc(o_ready, 1)

                def residual(c):
                    dve.wait_ge(ot_ps, NCH * g + c + 1)
                    dve.wait_ge(xres_landed[c], 16 * g + 16)
                    previous(dve, out_stored[c], 16 * g)
                    dve.tensor_tensor(outb[:, c], bank[7][:].rearrange("p (b n) -> p b n", n=P), xres[:, c],
                                      ALU.add).then_inc(out_ready, 1)

                if ahead:
                    h_low(g + 1, 0)
                reset(0)
                gated(0)
                update(0)
                if ahead:
                    h_low(g + 1, 1)
                reset(1)
                residual(0)
                if ahead:
                    level2(g + 1, 0)
                    v_low(g + 1, 0)
                gated(1)
                if ahead:
                    v_low(g + 1, 1)
                    v_low(g + 1, 2)
                update(1)
                if ahead:
                    left_rows(g + 1, 0)
                    left_rows(g + 1, 1)
                residual(1)

            lot_low(0)
            dve.wait_ge(pool_set, 5)
            dve.memset(right[64:67], -0.5).then_inc(pads_set, 1)
            h_low(0, 0)
            lot_low(1)
            h_low(0, 1)
            lot_low(2)
            dve.wait_ge(f1_ac, 2)
            n = LEN1["c"]
            dve.tensor_tensor(f1["b"][:, 0:n, :], f1["a"][:, 0:n, :], f1["c"], ALU.add).then_inc(f1_b, 1)
            dve.wait_ge(f1_b, 1)
            dve.tensor_tensor(fs["b"], f1["b"][:, 0:n:2, :], f1["b"][:, 1:n:2, :], ALU.add).then_inc(fs_b, 1)
            dve.wait_ge(seb_landed, 3 * 16)
            dve.wait_ge(bm_landed, 16)
            dve.wait_ge(pads_set, 9)
            level2(0, 0)
            for q in range(3):
                v_low(0, q)
            lot_low(plain)
            lot_low(plain + 1)
            for c in range(NCH):
                left_rows(0, c)
            for n in range(plain + 2, EARLY):
                lot_low(n)
            dve.wait_ge(gb_landed, 6 * 16)
            dve.tensor_tensor(par[:, HR:HR + 2], par[:, BIR:BIR + 2], par[:, BHR:BHR + 2],
                              ALU.add).then_inc(bias_set, 1)
            dve.tensor_scalar(par[:, HN:HN + 1], par[:, BHN:BHN + 1], 0.5, None, ALU.mult).then_inc(bias_set, 1)
            dve.wait_ge(bias_set, 2)
            dve.tensor_scalar(par[:, HR:HR + 2], par[:, HR:HR + 2], 0.5, None, ALU.mult).then_inc(bias_set, 1)
            body(0, True, first=True)
            with dve.Fori(1, NG - 1) as g:
                body(g, True)
            body(NG - 1, False)

        @block.tensor
        def _(pe):
            def three(dst, blk, hi, lo, start, stop):
                pe.matmul(dst, wt_hi[:, blk, :], hi, start=start, stop=False)
                pe.matmul(dst, wt_hi[:, blk, :], lo, start=False, stop=False)
                return pe.matmul(dst, wt_lo[:, blk, :], hi, start=False, stop=stop)

            def h_transpose(g, c):
                pe.wait_ge(hn_ready, NCH * g + c + 1)
                previous(pe, mbs_ready, 3 * g) if c == 0 else previous(pe, m_ready, 6 * g)
                for b in range(CB):
                    last = pe.transpose(bank[c][:, b * P:(b + 1) * P], hn[:, c, b, :], ident[:])
                last.then_inc(ht_ps, 1)

            def lot_transpose(n):
                before = [m for m in range(n) if LOT_BANK[m] == LOT_BANK[n]]
                if before:
                    pe.wait_ge(wt_lo_ready, before[-1] + 1)
                for i, blk in enumerate(lots[n]):
                    last = pe.transpose(bank[LOT_BANK[n]][:, i * P:(i + 1) * P], blocks[blk], ident[:])
                last.then_inc(wt_ps, 1)

            def sub_conv(g, q, first):
                at, n = SUBS[q]
                if first:
                    pe.wait_ge(wt_lo_ready, lot_of(at + n - 1) + 1)
                u, v = q // 3, q % 3
                if u == 0:
                    pe.wait_ge(v_lob_ready, 3 * g + q + 1)
                    if v == 2:
                        pe.wait_ge(msg_sum_ready, NCH * g + NCH)
                else:
                    pe.wait_ge(v_loac_ready, 6 * g + q - 2)
                    if v == 0:
                        previous(pe, mbs_ready, 3 * g + u)
                    else:
                        pe.wait_ge(m_ready, 6 * g + 2 * (u - 1) + v)
                dst = bank[v][:, 0:GB * QUART].rearrange("p (b l) -> p b l", l=QUART)
                for i in range(n):
                    last = three(dst, at + i, v_hi[:, q, :, i:i + QUART], v_lo[:, q, :, i:i + QUART],
                                 i == 0, i == n - 1)
                last.then_inc(conv2_ps, 1)

            def gates(g, c, ahead):
                cs = slice(c * CW, (c + 1) * CW)
                h = (h_hi[:, cs], h_lo[:, cs])
                nm = (n_hi[:, cs], n_lo[:, cs])
                xc = (xc_hi[:, cs], xc_lo[:, cs])
                pe.wait_ge(at_ready, NCH * g + NCH) if c == 0 else previous(pe, ghn_ready, NCH * g + c)
                three(bank[3][:], HH(N), *h, True, True).then_inc(ghn_ps, 1)
                pe.wait_ge(e_ready, NCH * g + NCH) if c == 0 else previous(pe, r_ready, NCH * g + c)
                three(bank[4][:], HH(R), *h, True, False)
                pe.wait_ge(m_ready, 6 * g + 6) if c else pe.wait_ge(n_lo_ready, NCH * g + 1)
                zb = bank[Z_BANK[c]][:]
                three(zb, HH(Z), *h, True, False).then_inc(h_used, 1)
                if ahead:
                    h_transpose(g + 1, c)
                pe.wait_ge(n_lo_ready, NCH * g + c + 1)
                three(bank[4][:], IH(R, 1), *nm, False, False)
                if c:
                    pe.wait_ge(v_ready, NCH * g + c)
                three(bank[5][:], IH(N, 1), *nm, True, False)
                three(zb, IH(Z, 1), *nm, False, False)
                pe.wait_ge(xc_lo_ready, NCH * g + c + 1)
                three(bank[4][:], IH(R, 0), *xc, False, True).then_inc(r_ps, 1)
                three(bank[5][:], IH(N, 0), *xc, False, True).then_inc(gin_ps, 1)
                three(zb, IH(Z, 0), *xc, False, True).then_inc(z_ps, 1)

            def out_transpose(g, c):
                pe.wait_ge(o_ready, NCH * g + c + 1)
                if c:
                    previous(pe, out_ready, NCH * g + c)
                for b in range(CB):
                    last = pe.transpose(bank[7][:, b * P:(b + 1) * P], gw[c][:, b * P:(b + 1) * P], ident[:])
                last.then_inc(ot_ps, 1)

            def a_transpose(g, c):
                pe.wait_ge(a_ready, NCH * g + c + 1)
                previous(pe, ghn_ready, NCH * g) if c == 0 else pe.wait_ge(at_ready, NCH * g + c)
                for b in range(CB):
                    last = pe.transpose(bank[3][:, b * P:(b + 1) * P], aff[:, c * CB + b, :], ident[:])
                last.then_inc(at_ps, 1)

            def gather(g, c):
                pe.wait_ge(msg_ready, NCH * g + c + 1)
                pe.wait_ge(at_ready, NCH * g + c + 1)
                if c:
                    previous(pe, out_ready, NCH * g)
                for b in range(CB):
                    last = pe.matmul(bank[6 + c][:, b * P:(b + 1) * P], msg[:, c * CB + b, :],
                                     aff_t[:, c * CB + b, :], start=True, stop=True)
                last.then_inc(nmp_ps, 1)

            def head(g, first=False):
                for c in range(NCH):
                    cs = slice(c * CW, (c + 1) * CW)
                    pe.wait_ge(h_lo_ready, NCH * g + c + 1)
                    three(bank[c][:], CONV1, h_hi[:, cs], h_lo[:, cs], True, True).then_inc(conv1_ps, 1)
                if first:
                    pe.wait_ge(wt_lo_ready, plain)
                for c in range(NCH):
                    cs = slice(c * CW, (c + 1) * CW)
                    previous(pe, r_ready, NCH * g) if c == 0 else previous(pe, v_ready, NCH * g)
                    dst = bank[4 + c][0:96, :]
                    pe.matmul(dst, wt_hi[:, SE, 0:96], h_hi[:, cs], start=True, stop=False)
                    pe.matmul(dst, wt_hi[:, SE, 0:96], h_lo[:, cs], start=False, stop=False)
                    pe.matmul(dst, wt_lo[:, SE, 0:96], h_hi[:, cs], start=False, stop=True).then_inc(s_ps, 1)
                if first:
                    pe.wait_ge(fs_b, 1)
                    pe.wait_ge(c_ready, NCH)
                    lot_transpose(plain)
                    lot_transpose(plain + 1)
                for c in range(NCH):
                    previous(pe, z_ready, NCH * (g - 1) + c + 1)
                    for b in range(CB):
                        hs = slice((c * CB + b) * P, (c * CB + b + 1) * P)
                        last = pe.matmul(bank[Z_BANK[c]][:, b * P:(b + 1) * P], hf[:, hs], wt_msg[:],
                                         start=True, stop=True)
                    last.then_inc(msg_ps, 1)

            def distance(g, c):
                pe.wait_ge(s_ready, NCH * g + c + 1)
                pe.wait_ge(sq_ready, 2 * (NCH * g + c + 1))
                pe.wait_ge(right_ready, NCH * g + c + 1)
                for b in range(CB):
                    last = pe.matmul(bank[4 + c][:, b * P:(b + 1) * P], left[:, c * CB + b, :],
                                     right[:, c * CB + b, :], start=True, stop=True)
                last.then_inc(dist_ps, 1)

            def body(g, ahead, first=False):
                for q in range(9):
                    sub_conv(g, q, first)
                    if q == 0 and not first:
                        out_transpose(g - 1, 1)
                    if first:
                        for n in {0: (0,), 1: (1, 2), 2: (3,), 3: (4, 5)}.get(q, ()):
                            lot_transpose(EARLY + n)
                    if first and q == 4:
                        pe.wait_ge(wt_lo_ready, len(lots))
                    if q == 1:
                        distance(g, 0)
                        distance(g, 1)
                    if q in (4, 5):
                        a_transpose(g, q - 4)
                    if q in (6, 7):
                        gather(g, q - 6)
                gates(g, 0, ahead)
                gates(g, 1, ahead)
                out_transpose(g, 0)
                if ahead:
                    head(g + 1)
                else:
                    out_transpose(g, 1)

            pe.wait_ge(ident_ready, 1)
            pe.wait_ge(ih_landed, 16)
            lot_transpose(0)
            h_transpose(0, 0)
            pe.wait_ge(w1_scaled, 1)
            pe.wait_ge(w_landed, 2 * 16)
            lot_transpose(1)
            h_transpose(0, 1)
            pe.wait_ge(se_landed, 3 * 16)
            lot_transpose(2)
            pe.wait_ge(wt_lo_ready, 2)
            head(0, first=True)
            pe.wait_ge(fs_ac, 2)
            for n in range(plain + 2, EARLY):
                lot_transpose(n)
            pe.wait_ge(pads_set, 9)
            body(0, True, first=True)
            with pe.Fori(1, NG - 1) as g:
                body(g, True)
            body(NG - 1, False)


def previous(engine, semaphore, count):
    if not isinstance(count, int) or count > 0:
        engine.wait_ge(semaphore, count)


_INS = ["x", "adj", "w_se", "b_se", "conv1_w", "bn1_g", "bn1_b", "bn1_m", "bn1_v", "conv2_w", "bn2_g", "bn2_b",
        "bn2_m", "bn2_v", "w_msg", "b_msg", "w_ih", "b_ih", "w_hh", "b_hh"]


def kernel(**inputs):
    import numpy as np
    import concourse.bacc as bacc
    from concourse.bass_utils import run_bass_kernel_spmd

    nc = bacc.Bacc("TRN2", target_bir_lowering=False, num_devices=1)
    arrays, args = {}, []
    for name in _INS:
        a = np.ascontiguousarray(inputs[name if name in ("x", "adj") else "L0_gnn_" + name])
        arrays[f"in_{name}"] = a
        args.append(nc.dram_tensor(f"in_{name}", a.shape, mybir.dt.from_np(a.dtype), kind="ExternalInput").ap())
    out = nc.dram_tensor("out", (NB, P, P), F32, kind="ExternalOutput").ap()
    gnn_kernel(nc, *args, out)
    return run_bass_kernel_spmd(nc, [arrays], core_ids=[0]).results[0]["out"]
```
